# Optimizing a Trainium2 kernel written in Bass

```python
import numpy as np
import jax
import jax.numpy as jnp

def _softmax(x, axis=-1):
    return jax.nn.softmax(x, axis=axis)

def _gelu(x):
    return jax.nn.gelu(x, approximate=True)

def _silu(x):
    return jax.nn.silu(x)

def _sigmoid(x):
    return jax.nn.sigmoid(x)

def _layernorm(x, axis=-1, eps=1e-05):
    m = jnp.mean(x, axis=axis, keepdims=True)
    v = jnp.var(x, axis=axis, keepdims=True)
    return (x - m) / jnp.sqrt(v + eps)

def _scatter_add(tgt, idx, src, axis=0):
    return tgt.at[idx].add(src)

def _segment_sum(src, seg, n):
    return jax.ops.segment_sum(src, seg, n)
kernel_name = 'mk_xattn_ffn_d1_seqx_r4_34466d'

def setup_inputs(seed: int=0):
    np.random.seed(seed)
    _w = jnp.asarray

    def _rec_inputs():
        import jax
        import jax.numpy as jnp
        _rk = jax.random.key(seed)
        x = -0.0002928 + 1 * jax.random.normal(jax.random.fold_in(_rk, 1), (1, 2048, 256), jnp.float32)
        _lenS = 2048 - jax.random.randint(jax.random.fold_in(_rk, 7), (1,), 0, max(1, 2048 // 4) + 1, jnp.int32)
        _lenS2 = 1601 - jax.random.randint(jax.random.fold_in(_rk, 8), (1,), 0, max(1, 1601 // 4) + 1, jnp.int32)
        _ctx_1024P = jax.random.normal(jax.random.fold_in(_rk, 11), (1, 16, 256), jnp.float32)
        _ctx_1024c = jax.random.dirichlet(jax.random.fold_in(_rk, 511), 0.3 * jnp.ones((16,), jnp.float32), (1, 1601))
        _ctx_1024t = jnp.einsum('bsk,bkd->bsd', _ctx_1024c, _ctx_1024P)
        _ctx_1024t = _ctx_1024t * jax.lax.rsqrt(jnp.mean(jnp.square(_ctx_1024t)) + 1e-12) * 0.953939
        ctx_1024 = -1.39393e-06 + 0.999914 * (_ctx_1024t + 0.3 * jax.random.normal(jax.random.fold_in(_rk, 611), (1, 1601, 256), jnp.float32))
        return (x, ctx_1024)
    x, ctx_1024 = _rec_inputs()

    def _L0_xattn_setup():
        import jax, jax.numpy as jnp
        import numpy as np
        MODEL_SIZE = 256
        H = 16
        KEY_SIZE = MODEL_SIZE // H
        key = jax.random.key(seed)
        ks = jax.random.split(key, 10)
        B, SQ, SK, D = (2, 512, 512, MODEL_SIZE)
        s = 1.0 / np.sqrt(D)
        return {'decoder_output': jax.random.normal(ks[0], (B, SQ, D), jnp.float32), 'encoder_output': jax.random.normal(ks[1], (B, SK, D), jnp.float32), 'wq': jax.random.normal(ks[2], (D, D), jnp.float32) * s, 'bq': jnp.zeros((D,), jnp.float32), 'wk': jax.random.normal(ks[3], (D, D), jnp.float32) * s, 'bk': jnp.zeros((D,), jnp.float32), 'wv': jax.random.normal(ks[4], (D, D), jnp.float32) * s, 'bv': jnp.zeros((D,), jnp.float32), 'wo': jax.random.normal(ks[5], (D, D), jnp.float32) * s, 'bo': jnp.zeros((D,), jnp.float32)}
    _L0_xattn_all = _L0_xattn_setup()
    _L0_xattn_in = {k: v for k, v in _L0_xattn_all.items() if k in ('wq', 'bq', 'wk', 'bk', 'wv', 'bv', 'wo', 'bo')}
    del _L0_xattn_all

    def _L0_ffn_setup():
        import jax, jax.numpy as jnp
        import numpy as np
        D_MODEL = 256
        D_FF = 1024
        NUM_EXPERTS = 8
        B, N = (16, 256)
        key = jax.random.key(seed)
        ks = jax.random.split(key, 7)
        s_in = 1.0 / np.sqrt(D_MODEL)
        s_ff = 1.0 / np.sqrt(D_FF)
        return {'x': jax.random.normal(ks[0], (B, N, D_MODEL), dtype=jnp.float32), 'Wr': jax.random.uniform(ks[1], (D_MODEL, NUM_EXPERTS), jnp.float32, -s_in, s_in), 'br': jax.random.uniform(ks[2], (NUM_EXPERTS,), jnp.float32, -s_in, s_in), 'W1': jax.random.uniform(ks[3], (NUM_EXPERTS, D_MODEL, D_FF), jnp.float32, -s_in, s_in), 'b1': jax.random.uniform(ks[4], (NUM_EXPERTS, D_FF), jnp.float32, -s_in, s_in), 'W2': jax.random.uniform(ks[5], (NUM_EXPERTS, D_FF, D_MODEL), jnp.float32, -s_ff, s_ff), 'b2': jax.random.uniform(ks[6], (NUM_EXPERTS, D_MODEL), jnp.float32, -s_ff, s_ff)}
    _L0_ffn_all = _L0_ffn_setup()
    _L0_ffn_in = {k: v for k, v in _L0_ffn_all.items() if k in ('Wr', 'br', 'W1', 'b1', 'W2', 'b2')}
    del _L0_ffn_all
    return {'x': x, 'ctx_1024': ctx_1024, 'L0_xattn_wq': _L0_xattn_in['wq'], 'L0_xattn_bq': _L0_xattn_in['bq'], 'L0_xattn_wk': _L0_xattn_in['wk'], 'L0_xattn_bk': _L0_xattn_in['bk'], 'L0_xattn_wv': _L0_xattn_in['wv'], 'L0_xattn_bv': _L0_xattn_in['bv'], 'L0_xattn_wo': _L0_xattn_in['wo'], 'L0_xattn_bo': _L0_xattn_in['bo'], 'L0_ffn_Wr': _L0_ffn_in['Wr'], 'L0_ffn_br': _L0_ffn_in['br'], 'L0_ffn_W1': _L0_ffn_in['W1'], 'L0_ffn_b1': _L0_ffn_in['b1'], 'L0_ffn_W2': _L0_ffn_in['W2'], 'L0_ffn_b2': _L0_ffn_in['b2']}

def reference(x, ctx_1024, L0_xattn_wq, L0_xattn_bq, L0_xattn_wk, L0_xattn_bk, L0_xattn_wv, L0_xattn_bv, L0_xattn_wo, L0_xattn_bo, L0_ffn_Wr, L0_ffn_br, L0_ffn_W1, L0_ffn_b1, L0_ffn_W2, L0_ffn_b2):
    import jax
    import jax.numpy as jnp

    def _L0_xattn_ref(decoder_output, encoder_output, wq, bq, wk, bk, wv, bv, wo, bo):
        import jax, jax.numpy as jnp
        import numpy as np
        MODEL_SIZE = 256
        H = 16
        KEY_SIZE = MODEL_SIZE // H
        B, SQ, D = decoder_output.shape
        SK = encoder_output.shape[1]
        q = decoder_output @ wq + bq
        k = encoder_output @ wk + bk
        v = encoder_output @ wv + bv
        q = q.reshape(B, SQ, H, KEY_SIZE).transpose(0, 2, 1, 3)
        k = k.reshape(B, SK, H, KEY_SIZE).transpose(0, 2, 1, 3)
        v = v.reshape(B, SK, H, KEY_SIZE).transpose(0, 2, 1, 3)
        scale = 1.0 / jnp.sqrt(jnp.asarray(KEY_SIZE, q.dtype))
        score = jnp.einsum('bhqd,bhkd->bhqk', q, k) * scale
        align = jax.nn.softmax(score, axis=-1)
        ctx = jnp.einsum('bhqk,bhkd->bhqd', align, v)
        ctx = ctx.transpose(0, 2, 1, 3).reshape(B, SQ, D)
        return ctx @ wo + bo

    def _L0_ffn_ref(x, Wr, br, W1, b1, W2, b2):
        import jax, jax.numpy as jnp
        import numpy as np
        D_MODEL = 256
        D_FF = 1024
        NUM_EXPERTS = 8
        B, N = (16, 256)
        scores = jnp.einsum('bh,he->be', x.mean(axis=1), Wr) + br
        top1 = jnp.argmax(scores, axis=-1)
        w1 = W1[top1]
        c1 = b1[top1]
        w2 = W2[top1]
        c2 = b2[top1]
        h = jax.nn.relu(jnp.einsum('bnh,bhf->bnf', x, w1) + c1[:, None, :])
        out = jnp.einsum('bnf,bfh->bnh', h, w2) + c2[:, None, :]
        return out
    x = x + _L0_xattn_ref(_layernorm(x, axis=-1), ctx_1024, L0_xattn_wq, L0_xattn_bq, L0_xattn_wk, L0_xattn_bk, L0_xattn_wv, L0_xattn_bv, L0_xattn_wo, L0_xattn_bo)
    x = x + _L0_ffn_ref(_layernorm(x, axis=-1), L0_ffn_Wr, L0_ffn_br, L0_ffn_W1, L0_ffn_b1, L0_ffn_W2, L0_ffn_b2)
    return x

_drawn_inputs = setup_inputs


def setup_inputs(seed=0):
    import zlib

    import numpy as np

    out = dict(_drawn_inputs(seed))
    spreads = {'L0_xattn_bq': (0.0, 0.417),
     'L0_xattn_bk': (0.0, 0.8),
     'L0_xattn_bv': (0.0, 0.1),
     'L0_xattn_bo': (0.0, 0.1)}
    factors = {'L0_ffn_b1': 4.585, 'L0_ffn_b2': 3.662}
    for name, (base, spread) in spreads.items():
        noise = np.random.default_rng([zlib.crc32(name.encode()), seed]).standard_normal(out[name].shape)
        drawn = base * np.exp(spread * noise) if base else spread * noise
        out[name] = jnp.asarray(drawn.astype(out[name].dtype))
    for name, factor in factors.items():
        out[name] = (out[name] * factor).astype(out[name].dtype)
    return out
```

```python
import concourse.bass as bass
from concourse import mybir
from contextlib import ExitStack


def cross_attention_then_expert_ffn(
    nc: bass.Bass,
    x_in: bass.AP,
    ctx_in: bass.AP,
    wq_in: bass.AP,
    bq_in: bass.AP,
    wk_in: bass.AP,
    bk_in: bass.AP,
    wv_in: bass.AP,
    bv_in: bass.AP,
    wo_in: bass.AP,
    bo_in: bass.AP,
    wr_in: bass.AP,
    br_in: bass.AP,
    w1_in: bass.AP,
    b1_in: bass.AP,
    w2_in: bass.AP,
    b2_in: bass.AP,
    out: bass.AP,
):
    fp32 = mybir.dt.float32
    bf16 = mybir.dt.bfloat16
    u32 = mybir.dt.uint32
    ALU = mybir.AluOpType
    ACT = mybir.ActivationFunctionType
    AX = mybir.AxisListType

    P = 128
    TOK, C = x_in.shape[1], x_in.shape[2]
    KEYS = ctx_in.shape[1]
    H = 16
    D = C // H
    HG = 4
    NG = H // HG
    HB = P // D
    CB = C // P
    QC = 512
    NC = TOK // QC
    TT = TOK // P
    TQ = QC // P
    KT = -(-KEYS // P)
    KLAST = KEYS - (KT - 1) * P
    E, FF = w1_in.shape[0], w1_in.shape[2]
    FT = FF // P
    EPS = 1e-5
    SCALE = float(D) ** -0.5
    COL = 32

    TERMS_Q = "hhmmlh"
    TERMS_K = "hmhmhl"
    NT = len(TERMS_Q)
    KR = NT * D
    ROWS = KR + 2

    KN = [401, 400, 400, 400]
    assert sum(KN) == KEYS
    KO = [sum(KN[:n]) for n in range(len(KN))]
    MW = 401
    MO = [0, 400, 800, 1200]
    assert MO[-1] + MW == KEYS and all(b - a <= MW for a, b in zip(MO, MO[1:]))

    PR = 4
    LAG = 3
    NE = 3
    SLOTS = NG * KT
    AHEAD = 1
    HELD = 4
    ORDER = "smsmvsms"

    ctx = ExitStack()
    with ctx:
        def sb(name, shape, dt=fp32):
            return ctx.enter_context(nc.sbuf_tensor(name, shape, dt))

        def sem(name):
            return ctx.enter_context(nc.semaphore(name))

        r_kq = sb("r_kq", [P, H * KEYS + NG * HG * QC], bf16)
        kpack = r_kq[:, 0:H * KEYS].rearrange("p (h k) -> p h k", h=H)
        qbuf = r_kq[:, H * KEYS:].rearrange("p (g j q) -> p g j q", g=NG, j=HG)
        hid = r_kq[:, 0:2 * FT * TOK].bitcast(fp32).rearrange("p (f t) -> p f t", f=FT)
        VW = D + 1
        v_all = sb("v_all", [P, KT, H * VW + COL - VW])
        r_p = sb("r_p", [P, PR * HG * QC])
        probs = r_p[:, :].rearrange("p (s j q) -> p s j q", s=PR, j=HG)
        a = 0
        ctx_rows = r_p[:, a:a + KT * C].rearrange("p (t c) -> p t c", t=KT)
        stage = r_p[:, a:a + 4 * QC].rearrange("p (s q) -> p s q", s=4)
        a += KT * C
        ctx_t = r_p[:, a:a + CB * KEYS].rearrange("p (b k) -> p b k", b=CB)
        a += CB * KEYS
        w_qkv = r_p[:, a:a + 3 * CB * C].rearrange("p (w b n) -> p w b n", w=3, b=CB)
        a += 3 * CB * C
        assert a <= PR * HG * QC
        w1_sb = r_p[:, 0:CB * FF].rearrange("p (b f) -> p b f", b=CB)
        w2_sb = r_p[:, CB * FF:CB * FF + FT * C].rearrange("p (f c) -> p f c", f=FT)
        r_q = sb("r_q", [P, 3 * CB * TOK], bf16)
        q_part = r_q[:, :].rearrange("p (s b t) -> p s b t", s=3, b=CB)
        xn2 = r_q[:, 0:2 * TT * C].bitcast(fp32).rearrange("p (t c) -> p t c", t=TT)
        r_c = sb("r_c", [P, CB * TOK + NG * QC])
        k_part = r_c[:, :].bitcast(bf16)[:, 0:3 * CB * KEYS].rearrange("p (s b k) -> p s b k", s=3, b=CB)
        att = r_c[:, 0:CB * TOK].rearrange("p (b t) -> p b t", b=CB)
        att_raw = r_c[:, CB * TOK:].rearrange("p (g q) -> p g q", g=NG)
        xs = sb("xs", [P, TT, C])
        xn_t = sb("xn_t", [P, CB, TOK])
        den = xn_t[0:H, 0, :]
        sel = sb("sel", [H, CB, P])
        wo_sb = sb("wo_sb", [P, CB, C])
        ident = sb("ident", [P, P])
        ident_b = sb("ident_b", [P, P], bf16)
        bq_sb = sb("bq_sb", [P, CB])
        bk_sb = sb("bk_sb", [P, CB])
        bv_sb = sb("bv_sb", [P, C])
        b_row = sb("b_row", [P, C])
        b1_sb = sb("b1_sb", [P, FT])
        b1_rows = sb("b1_rows", [FT, P])
        wr_sb = sb("wr_sb", [P, CB, E])
        br_sb = sb("br_sb", [1, E])
        st = sb("st", [P, TT, 6])
        mv = sb("mv", [P, TT, 2])
        sd = sb("sd", [P, TT])
        rstd = sb("rstd", [P, TT])
        eps_sb = sb("eps_sb", [P, 1])
        ones_sb = sb("ones_sb", [P, 1])
        half_max = sb("half_max", [P, NG, HG * TQ, 2])
        neg = sb("neg", [P, NG, HG * TQ])
        neg_part = sb("neg_part", [P, NG, 2, HG * TQ], bf16)
        neg_rows = sb("neg_rows", [2 * HG * TQ, NG, P], bf16)
        mean_sb = sb("mean_sb", [P, CB])
        logits = sb("logits", [1, E])
        top8 = sb("top8", [1, 8])
        top_at = sb("top_at", [1, 8], u32)

        k_dram = nc.dram_tensor("k_parts", (3, C, KEYS), bf16, kind="Internal").ap()
        q_dram = nc.dram_tensor("q_parts", (3, C, TOK), bf16, kind="Internal").ap()

        ps = ctx.enter_context(nc.psum_tensor("ps", [P, 8, 512], fp32))
        V_BANK = NE
        M_BANK = 4

        ctx_in_s = sem("ctx_loaded")
        wk_s = sem("wk_loaded")
        wv_s = sem("wv_loaded")
        wq_s = sem("wq_loaded")
        x_s = [sem(f"x_loaded{n}") for n in range(NC)]
        small_s = sem("small_loaded")
        wo_s = sem("wo_loaded")
        xr_s = sem("x_reloaded")
        ident_s = sem("ident_ready")
        sel_s = sem("selection_half_ready")
        fills_s = sem("fills_ready")
        dve_s = sem("dve_steps")
        pre_s = sem("pre_products")
        pre_a = sem("pre_taken_act")
        pre_v = sem("pre_taken_dve")
        stats_s = sem("stats_ready")
        sqrt_s = sem("sqrt_ready")
        xn_s = sem("xn_ready")
        high_s = sem("high_part_ready")
        parts_s = sem("parts_ready")
        kout_s = [sem(f"k_parts_stored{b}") for b in range(CB)]
        qout_s = [sem(f"q_parts_stored{n}") for n in range(NC)]
        q_s = [sem(f"q_loaded{g}") for g in range(NG)]
        rows_s = [sem(f"max_rows_loaded{g}") for g in range(NG)]
        left_s = [sem(f"region_left{g}") for g in range(NG)]
        score_s = sem("scores_ready")
        prob_s = sem("probs_ready")
        pv_s = sem("pv_done")
        att_s = sem("att_taken")
        mrow_s = sem("max_scores_ready")
        max_s = sem("max_scores_taken")
        neg_s = sem("neg_max_steps")
        split_s = sem("neg_max_split")
        rec_s = sem("rden_ready")
        norm_s = sem("att_normalised")
        xb_s = sem("residual_biased")
        res_s = sem("residual_done")
        close_s = sem("close_products")
        taken_s = sem("close_taken")
        xn2_s = sem("xn2_ready")
        tail_s = sem("tail_products")
        tail_a = sem("tail_taken_act")
        tail_v = sem("tail_taken_dve")
        sum_s = sem("token_sum_ready")
        mean_s = sem("mean_ready")
        logit_s = sem("logits_ready")
        top_s = sem("top_ready")
        w1_s = sem("w1_loaded")
        b1_s = sem("b1_loaded")
        b1t_s = sem("b1_turned")
        b1c_s = sem("b1_column_ready")
        w2_s = sem("w2_loaded")
        b2_s = sem("b2_loaded")
        xb2_s = sem("residual2_biased")
        y_s = sem("y_products")
        out_s = sem("out_ready")
        stored_s = sem("stored")

        block = ctx.enter_context(nc.Block())

        ctx_groups = [range(4 * n, min(4 * n + 4, KT)) for n in range(-(-KT // 4))]

        PRE = [("ctx_t", n, b) for n in range(len(ctx_groups)) for b in range(CB)]
        PRE += [("k", n, b) for b in range(CB) for n in range(len(KN))]
        PRE += [("v", n, 0) for n in range(KT)]
        for n in range(NC):
            PRE += [("x_t", n, b) for b in range(CB)]
            PRE += [("q", n, b) for b in range(CB)]

        def by_act(item):
            return item[0] in ("k", "q") or (item[0] in ("ctx_t", "x_t") and item[2] == 0)

        def taken_before(i, act):
            return sum(by_act(x) == act for x in PRE[:i + 1])

        def pre_at(kind, n, b):
            return PRE.index((kind, n, b))

        def wait_taken(eng, i):
            act = by_act(PRE[i])
            eng.wait_ge(pre_a if act else pre_v, taken_before(i, act))

        STAGED = [x for x in PRE if x[0] in ("k", "q")]

        def plan(first, last):
            items, turn, wait = [], None, 0
            for n in range(first, last):
                for t in range(TQ):
                    for half in range(2):
                        items.append((n // HG, n % HG, t, half))
                        if turn is not None:
                            wait -= 1
                            if wait == 0:
                                items.append((turn, "turn"))
                                turn = None
                if n % HG == HG - 1:
                    turn, wait = n // HG, 2
            if turn is not None:
                items.append((turn, "turn"))
            return items

        FIRST = plan(0, HG + AHEAD)
        CHUNK = plan(HG + AHEAD, HG + AHEAD + NG * HG)
        FINAL = plan(HG + AHEAD, NG * HG)
        NFIRST, NCHUNK = len(FIRST), len(CHUNK)
        assert NCHUNK % 2 == 0

        def m_bank(n):
            return M_BANK + 2 * (n % 2)

        CLOSE = [("spread", 0, 0), ("spread", 0, 1)]
        for n in range(NC):
            if n + 1 < NC - 1:
                CLOSE += [("spread", n + 1, b) for b in range(CB)]
            if n == NC - 1:
                EARLY = len(CLOSE)
                CLOSE += [("spread", n, b) for b in range(CB)]
            CLOSE += [("project", t, 0) for t in range(n * TQ, (n + 1) * TQ)]

        def turn_at(items, unit):
            return items.index((unit, "turn"))

        def turned_keys(n):
            return sum(min(P, KEYS - t * P) for t in ctx_groups[n])

        def span(kind, n):
            return (KO[n], KN[n]) if kind == "k" else (n * QC, QC)

        @block.sync
        def _(sp):
            sp.dma_start(ctx_rows[:, 0:KT - 1, :],
                         ctx_in[0, 0:(KT - 1) * P, :].rearrange("(t p) c -> p t c", p=P)).then_inc(ctx_in_s, 16)
            sp.dma_start(ctx_rows[0:KLAST, KT - 1, :], ctx_in[0, (KT - 1) * P:KEYS, :]).then_inc(ctx_in_s, 16)
            sp.dma_start(w_qkv[:, 1, :, :], wk_in.rearrange("(b p) n -> p b n", p=P)).then_inc(wk_s, 16)
            xr = x_in[0].rearrange("(t p) c -> p t c", p=P)
            for n in range(NC):
                sp.dma_start(xs[:, n * TQ:(n + 1) * TQ, :], xr[:, n * TQ:(n + 1) * TQ, :]).then_inc(x_s[n], 16)
            sp.dma_start(w_qkv[:, 2, :, :], wv_in.rearrange("(b p) n -> p b n", p=P)).then_inc(wv_s, 16)
            sp.dma_start(w_qkv[:, 0, :, :], wq_in.rearrange("(b p) n -> p b n", p=P)).then_inc(wq_s, 16)
            sp.dma_start(wo_sb[:, :, :], wo_in.rearrange("(b p) n -> p b n", p=P)).then_inc(wo_s, 16)

            for b in range(CB):
                sp.wait_ge(parts_s, (b + 1) * len(KN))
                sp.dma_start(k_dram[:, b * P:(b + 1) * P, :].rearrange("s r k -> r s k"),
                             k_part[:, :, b, :]).then_inc(kout_s[b], 16)
                sp.wait_ge(kout_s[b], 16)
                for g in range(b * HB // HG, (b + 1) * HB // HG):
                    for t, part in enumerate(TERMS_K):
                        src = k_dram["hml".index(part), g * HG * D:(g + 1) * HG * D, :]
                        sp.dma_start(kpack[t * D:(t + 1) * D, g * HG:(g + 1) * HG, :],
                                     src.rearrange("(j d) k -> d j k", j=HG)).then_inc(left_s[g], 16)

            def load_q(g, col):
                for t, part in enumerate(TERMS_Q):
                    src = q_dram["hml".index(part), g * HG * D:(g + 1) * HG * D, bass.ds(col, QC)]
                    sp.dma_start(qbuf[t * D:(t + 1) * D, g, :, :],
                                 src.rearrange("(j d) q -> d j q", j=HG)).then_inc(q_s[g], 16)

            def load_rows(g):
                for s in range(2):
                    sp.dma_start(qbuf[KR + s:KR + s + 1, g, :, :].rearrange("a j (t q) -> a (j t) q", t=TQ),
                                 neg_rows[s * HG * TQ:(s + 1) * HG * TQ, g, :]).then_inc(rows_s[g], 16)

            def move_att(g, col):
                b, r = divmod(g * HG, HB)
                for j in range(HG):
                    sp.dma_start(att[(r + j) * D:(r + j + 1) * D, b, bass.ds(col, QC)],
                                 att_raw[j * COL:j * COL + D, g, :]).then_inc(left_s[g], 16)
                sp.dma_start(den[g * HG:(g + 1) * HG, bass.ds(col, QC)],
                             att_raw[D::COL, g, :]).then_inc(left_s[g], 16)

            for n in range(NC):
                sp.wait_ge(parts_s, CB * len(KN) + CB * (n + 1))
                cols = slice(n * QC, (n + 1) * QC)
                for b in range(CB):
                    sp.dma_start(q_dram[:, b * P:(b + 1) * P, cols].rearrange("s r q -> r s q"),
                                 q_part[:, :, b, cols]).then_inc(qout_s[n], 16)
                if n == 0:
                    sp.wait_ge(qout_s[0], CB * 16)
                    for g in range(NG):
                        load_q(g, 0)
            for n in range(1, NC):
                sp.wait_ge(qout_s[n], CB * 16)
            sp.wait_ge(max_s, turn_at(FIRST, 0) + 1)
            load_rows(0)
            for g in range(NG):
                sp.wait_ge(left_s[g], NT * 16)

            def chunk(c, last):
                for g in range(NG):
                    if g:
                        if not last:
                            sp.wait_ge(score_s, c * (SLOTS * HG) + g * KT * HG)
                            load_q(g - 1, c * QC + QC)
                        sp.wait_ge(att_s, c * NG + g + 1)
                        move_att(g - 1, c * QC)
                    if not (last and g == NG - 1):
                        sp.wait_ge(max_s, c * NCHUNK + NFIRST + turn_at(FINAL if last else CHUNK, g + 1) + 1)
                        load_rows((g + 1) % NG)
                if not last:
                    sp.wait_ge(score_s, c * (SLOTS * HG) + SLOTS * HG)
                    load_q(NG - 1, c * QC + QC)
                sp.wait_ge(att_s, c * NG + NG + 1)
                move_att(NG - 1, c * QC)

            with sp.Fori(0, NC - 1) as c:
                chunk(c, False)
            chunk(NC - 1, True)

            sp.wait_ge(pv_s, NC * SLOTS + 1)
            sp.wait_ge(top_s, 1)
            e = sp.value_load(top_at[0:1, 0:1], min_val=0, max_val=E - 1)
            sp.dma_start(b1_rows[:, :], b1_in[bass.ds(e, 1), :].rearrange("a (f p) -> (a f) p", p=P)).then_inc(b1_s, 16)
            sp.dma_start(w1_sb, w1_in[bass.ds(e, 1), :, :].rearrange("a (b p) f -> p (a b) f", p=P)).then_inc(w1_s, 16)
            sp.dma_start(w2_sb, w2_in[bass.ds(e, 1), :, :].rearrange("a (f p) n -> p (a f) n", p=P)).then_inc(w2_s, 16)
            sp.wait_ge(xb_s, TT)
            sp.dma_start(b_row[:, :], b2_in[bass.ds(e, 1), :].broadcast_to([P, C])).then_inc(b2_s, 16)
            outr = out[0].rearrange("(t p) c -> p t c", p=P)
            for t in range(TT):
                sp.wait_ge(out_s, t + 1)
                sp.dma_start(outr[:, t, :], xs[:, t, :]).then_inc(stored_s, 16)
            sp.wait_ge(stored_s, TT * 16)

        @block.gpsimd
        def _(pool):
            pool.memset(ident[:, :], 0.0).then_inc(ident_s, 1)
            pool.memset(ident_b[:, :], 0.0).then_inc(ident_s, 1)
            pool.wait_ge(ident_s, 2)
            for m in (ident, ident_b):
                pool.affine_select(out=m[:, :], in_=m[:, :], compare_op=ALU.not_equal, fill=1.0, base=0,
                                   pattern=[[-1, P]], channel_multiplier=1).then_inc(ident_s, 1)
            pool.memset(sel[:, :, :], 1.0).then_inc(ident_s, 1)
            for b in range(CB):
                s_b = sel[:, b, :]
                pool.wait_ge(ident_s, 5 + b)
                pool.affine_select(out=s_b, in_=s_b, compare_op=ALU.is_ge, fill=0.0, base=D * b * HB,
                                   pattern=[[1, P]], channel_multiplier=-D).then_inc(sel_s, 1)
                pool.wait_ge(sel_s, b + 1)
                pool.affine_select(out=s_b, in_=s_b, compare_op=ALU.is_ge, fill=0.0, base=D - 1 - D * b * HB,
                                   pattern=[[-1, P]], channel_multiplier=D).then_inc(ident_s, 1)
            pool.memset(eps_sb[:, :], EPS).then_inc(fills_s, 1)
            pool.memset(ones_sb[:, :], 1.0).then_inc(fills_s, 1)
            pool.memset(v_all[:, :, :], 1.0).then_inc(fills_s, 1)
            pool.wait_ge(fills_s, 3)
            pool.memset(kpack[KR:ROWS, :, :], 1.0).then_inc(fills_s, 1)
            pool.wait_ge(pre_s, len(PRE))
            pool.dma_start(xs[:, :, :], x_in[0].rearrange("(t p) c -> p t c", p=P)).then_inc(xr_s, 16)
            pool.wait_ge(xr_s, 16)
            pool.wait_ge(small_s, 96)
            pool.wait_ge(fills_s, 4)
            for t in range(TT):
                pool.tensor_tensor(xs[:, t, :], xs[:, t, :], b_row[:, :], ALU.add).then_inc(xb_s, 1)

            pool.wait_ge(b2_s, 16)
            pool.wait_ge(xn2_s, TT)
            for t in range(TT):
                pool.tensor_tensor(xs[:, t, :], xs[:, t, :], b_row[:, :], ALU.add).then_inc(xb2_s, 1)

        @block.scalar
        def _(act):
            act.dma_start(bk_sb[:, :], bk_in.rearrange("(b p) -> p b", p=P),
                          allow_slow_non_contiguous=True).then_inc(small_s, 16)
            act.dma_start(bq_sb[:, :], bq_in.rearrange("(b p) -> p b", p=P),
                          allow_slow_non_contiguous=True).then_inc(small_s, 16)
            act.dma_start(bv_sb[:, :], bv_in.partition_broadcast(P)).then_inc(small_s, 16)
            act.dma_start(b_row[:, :], bo_in.partition_broadcast(P)).then_inc(small_s, 16)
            act.dma_start(wr_sb[:, :, :], wr_in.rearrange("(b p) e -> p b e", p=P)).then_inc(small_s, 16)
            act.dma_start(br_sb[:, :], br_in.rearrange("(a e) -> a e", a=1)).then_inc(small_s, 16)
            act.wait_ge(fills_s, 1)
            act.wait_ge(stats_s, TT)
            act.activation(sd[:, :], mv[:, :, 1], ACT.Sqrt, bias=eps_sb[:, 0:1]).then_inc(sqrt_s, 1)
            act.wait_ge(small_s, 96)
            staged = 0
            for i, (kind, n, b) in enumerate(PRE):
                if not by_act(PRE[i]):
                    continue
                act.wait_ge(pre_s, i + 1)
                bank = i % 8
                if kind == "ctx_t":
                    act.activation(ctx_t[:, b, n * 512:n * 512 + turned_keys(n)], ps[:, bank, 0:turned_keys(n)],
                                   ACT.Copy).then_inc(pre_a, 1)
                elif kind == "x_t":
                    act.activation(xn_t[:, b, n * QC:(n + 1) * QC], ps[:, bank, :], ACT.Copy).then_inc(pre_a, 1)
                else:
                    part, bias = (k_part, bk_sb) if kind == "k" else (q_part, bq_sb)
                    o, w = span(kind, n)
                    if staged >= 4:
                        act.wait_ge(parts_s, staged - 3)
                    act.activation(stage[:, staged % 4, 0:w], ps[:, bank, 0:w], ACT.Identity,
                                   bias=bias[:, b:b + 1]).then_inc(pre_a, 1)
                    act.wait_ge(pre_a, taken_before(i, True))
                    act.activation(part[:, 0, b, o:o + w], stage[:, staged % 4, 0:w], ACT.Copy).then_inc(high_s, 1)
                    staged += 1
            act.sem_inc(att_s, 1)

            def take_att(c, g):
                act.wait_ge(pv_s, c * SLOTS + (g + 1) * KT + 1)
                act.wait_ge(left_s[g], c * (HG + 1) * 16 + NT * 16)
                act.activation(att_raw[:, g, :], ps[:, V_BANK, :], ACT.Copy).then_inc(att_s, 1)

            def chunk(c):
                for s in range(SLOTS):
                    g, kt = divmod(s, KT)
                    rows = P if kt < KT - 1 else KLAST
                    if g and kt == LAG:
                        take_att(c, g - 1)
                    act.wait_ge(pv_s, c * SLOTS + max(0, s - PR + 1) + 1)
                    for j in range(HG):
                        e = s * HG + j
                        act.wait_ge(score_s, c * (SLOTS * HG) + e + 1)
                        act.activation(probs[0:rows, s % PR, j, :], ps[0:rows, e % NE, :], ACT.Exp,
                                       scale=SCALE).then_inc(prob_s, 1)
                take_att(c, NG - 1)

            with act.Fori(0, NC - 1) as c:
                chunk(c)
            chunk(NC - 1)

            act.wait_ge(stats_s, 2 * TT)
            act.activation(sd[:, :], mv[:, :, 1], ACT.Sqrt, bias=eps_sb[:, 0:1]).then_inc(sqrt_s, 1)
            for i in range(0, CB * NC, 2):
                act.wait_ge(tail_s, i + 1)
                act.activation(xn_t[:, 0, (i // 2) * QC:(i // 2 + 1) * QC], ps[:, i % 4, :],
                               ACT.Copy).then_inc(tail_a, 1)
            act.wait_ge(b1c_s, 1)
            for i in range(0, NC * FT, 2):
                c, f = divmod(i, FT)
                act.wait_ge(tail_s, CB * NC + i + 1)
                act.activation(hid[:, f, c * QC:(c + 1) * QC], ps[:, i % 4, :], ACT.Relu,
                               bias=b1_sb[:, f:f + 1]).then_inc(tail_a, 1)

        @block.vector
        def _(dve):
            steps = [0]

            def link(ins):
                steps[0] += 1
                ins.then_inc(dve_s, 1)
                dve.wait_ge(dve_s, steps[0])

            def take_pre(i):
                kind, n, b = PRE[i]
                dve.wait_ge(pre_s, i + 1)
                bank = i % 8
                if kind == "ctx_t":
                    dve.tensor_copy(ctx_t[:, b, n * 512:n * 512 + turned_keys(n)],
                                    ps[:, bank, 0:turned_keys(n)]).then_inc(pre_v, 1)
                elif kind == "x_t":
                    dve.tensor_copy(xn_t[:, b, n * QC:(n + 1) * QC], ps[:, bank, :]).then_inc(pre_v, 1)
                else:
                    rows = P if n < KT - 1 else KLAST
                    dve.tensor_tensor(v_all[0:rows, n, 0:H * VW].rearrange("p (h w) -> p h w", w=VW)[:, :, 0:D],
                                      ps[0:rows, bank, 0:C].rearrange("p (h d) -> p h d", h=H),
                                      bv_sb[0:rows, :].rearrange("p (h d) -> p h d", h=H),
                                      ALU.add).then_inc(pre_v, 1)

            def split_parts(i):
                kind, n, b = STAGED[i]
                o, w = span(kind, n)
                part = k_part if kind == "k" else q_part
                s = stage[:, i % 4, 0:w]
                dve.wait_ge(high_s, i + 1)
                link(dve.tensor_tensor(s, s, part[:, 0, b, o:o + w], ALU.subtract))
                link(dve.tensor_copy(part[:, 1, b, o:o + w], s))
                dve.tensor_tensor(part[:, 2, b, o:o + w], s, part[:, 1, b, o:o + w],
                                  ALU.subtract).then_inc(parts_s, 1)

            for n in range(NC):
                dve.wait_ge(x_s[n], 16)
                for t in range(n * TQ, (n + 1) * TQ):
                    last = dve.bn_stats(st[:, t, :], xs[:, t, :])
            link(last)
            for t in range(TT):
                dve.bn_aggr(mv[:, t, :], st[:, t, :]).then_inc(stats_s, 1)
            dve.wait_ge(sqrt_s, 1)
            link(dve.reciprocal(rstd[:, :], sd[:, :]))
            for t in range(TT):
                dve.tensor_scalar(xs[:, t, :], xs[:, t, :], mv[:, t, 0:1], rstd[:, t:t + 1],
                                  ALU.subtract, ALU.mult).then_inc(xn_s, 1)
            dve.wait_ge(small_s, 96)
            dve.wait_ge(fills_s, 3)
            staged = 0
            for i, item in enumerate(PRE):
                if item[0] in ("k", "q"):
                    split_parts(staged)
                    staged += 1
                elif not by_act(item):
                    take_pre(i)

            def take_max(c, n, item):
                unit, g = item[0], item[0] % NG
                dve.wait_ge(mrow_s, c * NCHUNK + n + 1)
                bank = m_bank(n)
                if item[1] == "turn":
                    dve.tensor_copy(neg_rows[:, g, :],
                                    ps[0:2 * HG * TQ, bank, 0:P // 2].bitcast(bf16)).then_inc(max_s, 1)
                    return
                _, j, t, half = item
                dve.reduce_max(half_max[:, g, j * TQ + t, half:half + 1], ps[:, bank:bank + 2, 0:MW],
                               AX.XY).then_inc(max_s, 1)
                if (j, t, half) == (HG - 1, TQ - 1, 1):
                    dve.wait_ge(max_s, c * NCHUNK + n + 1)
                    dve.tensor_reduce(neg[:, g, :], half_max[:, g, :, :], AX.X, ALU.max,
                                      negate=True).then_inc(neg_s, 1)
                    dve.wait_ge(neg_s, c * (2 * NG) + 2 * unit + 1)
                    dve.tensor_copy(neg_part[:, g, 0, :], neg[:, g, :]).then_inc(neg_s, 1)
                    dve.wait_ge(neg_s, c * (2 * NG) + 2 * unit + 2)
                    dve.tensor_tensor(neg_part[:, g, 1, :], neg[:, g, :], neg_part[:, g, 0, :],
                                      ALU.subtract).then_inc(split_s, 1)

            def invert(n):
                for g in range(NG):
                    dve.wait_ge(left_s[g], NT * 16 + (n + 1) * (HG + 1) * 16)
                dve.reciprocal(den[:, n * QC:(n + 1) * QC], den[:, n * QC:(n + 1) * QC]).then_inc(rec_s, 1)

            for n, item in enumerate(FIRST):
                take_max(0, n, item)
            with dve.Fori(0, NC - 1) as c:
                for n, item in enumerate(CHUNK):
                    take_max(c, NFIRST + n, item)
            for n, item in enumerate(FINAL):
                take_max(NC - 1, NFIRST + n, item)
                if n % 20 == 19 and n // 20 < NC - 1:
                    invert(n // 20)

            for k, (kind, n, b) in enumerate(CLOSE):
                if (kind, n, b) == ("spread", NC - 1, 0):
                    invert(NC - 1)
                dve.wait_ge(close_s, k + 1)
                bank = M_BANK + k % 4
                if kind == "spread":
                    cols = slice(n * QC, (n + 1) * QC)
                    dve.tensor_tensor(att[:, b, cols], att[:, b, cols], ps[:, bank, :], ALU.mult).then_inc(taken_s, 1)
                else:
                    dve.wait_ge(xb_s, n + 1)
                    dve.tensor_tensor(xs[:, n, :], ps[:, bank, 0:C], xs[:, n, :], ALU.add).then_inc(taken_s, 1)
                    dve.wait_ge(taken_s, k + 1)
                    link(dve.bn_stats(st[:, n, :], xs[:, n, :]))
                    dve.bn_aggr(mv[:, n, :], st[:, n, :]).then_inc(stats_s, 1)
            dve.wait_ge(sqrt_s, 2)
            link(dve.reciprocal(rstd[:, :], sd[:, :]))
            for g in range(NG):
                dve.wait_ge(q_s[g], NC * NT * 16)
            for t in range(TT):
                dve.tensor_scalar(xn2[:, t, :], xs[:, t, :], mv[:, t, 0:1], rstd[:, t:t + 1],
                                  ALU.subtract, ALU.mult).then_inc(xn2_s, 1)
            for i in range(1, CB * NC, 2):
                dve.wait_ge(tail_s, i + 1)
                dve.tensor_copy(xn_t[:, 1, (i // 2) * QC:(i // 2 + 1) * QC], ps[:, i % 4, :]).then_inc(tail_v, 1)
            dve.wait_ge(sum_s, 1)
            dve.tensor_scalar(mean_sb[:, :], ps[:, M_BANK:M_BANK + CB, 0], 1.0 / TOK, None,
                              ALU.mult).then_inc(mean_s, 1)
            dve.wait_ge(logit_s, 1)
            link(dve.tensor_tensor(logits[:, :], ps[0:1, M_BANK + CB, 0:E], br_sb[:, :], ALU.add))
            link(dve.max(top8[:, :], logits[:, :]))
            dve.max_index(top_at[:, :], top8[:, :], logits[:, :]).then_inc(top_s, 1)

            def hidden(c):
                for f in range(1, FT, 2):
                    i = CB * NC + c * FT + f
                    dve.wait_ge(tail_s, i + 1)
                    dve.tensor_scalar(hid[:, f, c * QC:(c + 1) * QC], ps[:, i % 4, :], b1_sb[:, f:f + 1], 0.0,
                                      ALU.add, ALU.max).then_inc(tail_v, 1)

            def result(c):
                for t in range(c * TQ, (c + 1) * TQ):
                    dve.wait_ge(y_s, t + 1)
                    dve.wait_ge(xb2_s, t + 1)
                    dve.tensor_tensor(xs[:, t, :], ps[:, M_BANK + t % 4, 0:C], xs[:, t, :],
                                      ALU.add).then_inc(out_s, 1)

            dve.wait_ge(b1t_s, 1)
            dve.tensor_copy(b1_sb[:, :], ps[:, M_BANK + 3, 0:FT]).then_inc(b1c_s, 1)
            dve.wait_ge(b1c_s, 1)
            for c in range(NC):
                hidden(c)
                if c:
                    result(c - 1)
            result(NC - 1)

        @block.tensor
        def _(pe):
            def turn_rows(bank, src, tiles, rows_of):
                for k, t in enumerate(tiles):
                    r = rows_of(t)
                    last = pe.transpose(ps[:, bank, k * P:k * P + r], src(t, r), ident[0:r, 0:r])
                return last

            pe.wait_ge(ident_s, 4)
            for i, (kind, n, b) in enumerate(PRE):
                if i >= 8:
                    wait_taken(pe, i - 8)
                bank = i % 8
                if kind == "ctx_t":
                    pe.wait_ge(ctx_in_s, 32)
                    last = turn_rows(bank, lambda t, r: ctx_rows[0:r, t, b * P:(b + 1) * P], ctx_groups[n],
                                     lambda t: min(P, KEYS - t * P))
                elif kind == "k":
                    pe.wait_ge(wk_s, 16)
                    wait_taken(pe, pre_at("ctx_t", len(ctx_groups) - 1, 0))
                    wait_taken(pe, pre_at("ctx_t", len(ctx_groups) - 1, 1))
                    o, w = span(kind, n)
                    for kb in range(CB):
                        last = pe.matmul(ps[:, bank, 0:w], w_qkv[:, 1, kb, b * P:(b + 1) * P],
                                         ctx_t[:, kb, o:o + w], start=(kb == 0), stop=(kb == CB - 1))
                elif kind == "v":
                    pe.wait_ge(wv_s, 16)
                    rows = P if n < KT - 1 else KLAST
                    for kb in range(CB):
                        last = pe.matmul(ps[0:rows, bank, 0:C], ctx_t[:, kb, n * P:n * P + rows],
                                         w_qkv[:, 2, kb, :], start=(kb == 0), stop=(kb == CB - 1))
                elif kind == "x_t":
                    pe.wait_ge(xn_s, (n + 1) * TQ)
                    last = turn_rows(bank, lambda t, r: xs[:, t, b * P:(b + 1) * P],
                                     range(n * TQ, (n + 1) * TQ), lambda t: P)
                else:
                    pe.wait_ge(wq_s, 16)
                    wait_taken(pe, pre_at("x_t", n, 0))
                    wait_taken(pe, pre_at("x_t", n, 1))
                    for kb in range(CB):
                        last = pe.matmul(ps[:, bank, :], w_qkv[:, 0, kb, b * P:(b + 1) * P],
                                         xn_t[:, kb, n * QC:(n + 1) * QC], start=(kb == 0), stop=(kb == CB - 1))
                last.then_inc(pre_s, 1)
            for i in range(len(PRE) - 8, len(PRE)):
                wait_taken(pe, i)
            pe.sem_inc(pv_s, 1)

            def max_scores(c, n, item):
                unit, g = item[0], item[0] % NG
                if not (isinstance(c, int) and c * NCHUNK + n < 2):
                    pe.wait_ge(max_s, c * NCHUNK + n - 1)
                bank = m_bank(n)
                if item[1] == "turn":
                    pe.wait_ge(split_s, c * NG + unit + 1)
                    pe.transpose(ps[0:2 * HG * TQ, bank, 0:P // 2].bitcast(bf16),
                                 neg_part[:, g, :, :].rearrange("p s n -> p (s n)"), ident_b[:, :]).then_inc(mrow_s, 1)
                    return
                _, j, t, half = item
                if (j, t, half) == (0, 0, 0):
                    pe.wait_ge(q_s[g], c * (NT * 16) + (unit // NG + 1) * NT * 16)
                for k in range(2):
                    o = MO[2 * half + k]
                    last = pe.matmul(ps[:, bank + k, 0:MW], qbuf[0:KR, g, j, t * P:(t + 1) * P],
                                     kpack[0:KR, g * HG + j, o:o + MW], start=True, stop=True)
                last.then_inc(mrow_s, 1)

            def scores(c, s, j):
                g, kt = divmod(s, KT)
                rows = P if kt < KT - 1 else KLAST
                if kt == 0 and j == 0:
                    pe.wait_ge(rows_s[g], c * 32 + 32)
                e = s * HG + j
                if e >= NE:
                    pe.wait_ge(prob_s, c * (SLOTS * HG) + e - NE + 1)
                pe.matmul(ps[0:rows, e % NE, :], kpack[0:ROWS, g * HG + j, kt * P:kt * P + rows],
                          qbuf[0:ROWS, g, j, :], start=True, stop=True).then_inc(score_s, 1)

            def times_v(c, s):
                g, kt = divmod(s, KT)
                rows = P if kt < KT - 1 else KLAST
                if kt == 0:
                    pe.wait_ge(att_s, c * NG + g + 1)
                pe.wait_ge(prob_s, c * (SLOTS * HG) + (s + 1) * HG)
                for j in range(HG):
                    last = pe.matmul(ps[j * COL:(j + 1) * COL, V_BANK, :], v_all[0:rows, kt, (g * HG + j) * VW:(g * HG + j) * VW + COL],
                                     probs[0:rows, s % PR, j, :], start=(kt == 0), stop=(kt == KT - 1))
                last.then_inc(pv_s, 1)

            def close(k):
                kind, n, b = CLOSE[k]
                bank = M_BANK + k % 4
                if k < 4:
                    pe.wait_ge(max_s, (NC - 1) * NCHUNK + NFIRST + len(FINAL))
                else:
                    pe.wait_ge(taken_s, k - 3)
                if kind == "spread":
                    pe.wait_ge(ident_s, 5 + CB)
                    pe.wait_ge(rec_s, n + 1)
                    last = pe.matmul(ps[:, bank, :], sel[:, b, :], den[:, n * QC:(n + 1) * QC], start=True, stop=True)
                else:
                    pe.wait_ge(wo_s, 16)
                    pe.wait_ge(taken_s, CLOSE.index(("spread", n // TQ, CB - 1)) + 1)
                    for b in range(CB):
                        last = pe.matmul(ps[:, bank, 0:C], att[:, b, n * P:(n + 1) * P], wo_sb[:, b, :],
                                         start=(b == 0), stop=(b == CB - 1))
                last.then_inc(close_s, 1)

            def chunk(c, items, late):
                done, over, held = 0, late or SLOTS, 0 if late else HELD
                for s in range(SLOTS):
                    for k, what in enumerate(ORDER):
                        if what == "s":
                            scores(c, s, ORDER[:k].count("s"))
                        elif what == "v" and s >= LAG:
                            times_v(c, s - LAG)
                        elif what == "m":
                            place = ORDER.count("m") * s + ORDER[:k].count("m") + 1
                            upto = min(len(items), (len(items) - held) * place // (ORDER.count("m") * over))
                            for n in range(done, upto):
                                max_scores(c, NFIRST + n, items[n])
                            done = max(done, upto)
                    if late:
                        first = SLOTS - 12
                        for k in range(max(0, EARLY * (s - first) // 12), max(0, EARLY * (s + 1 - first) // 12)):
                            close(k)
                for s in range(SLOTS - LAG, SLOTS):
                    upto = len(items) if s == SLOTS - 1 else done + (len(items) - done) // (SLOTS - s)
                    for n in range(done, upto):
                        max_scores(c, NFIRST + n, items[n])
                    done = upto
                    times_v(c, s)

            for g in range(NG):
                pe.wait_ge(left_s[g], NT * 16)
            pe.wait_ge(fills_s, 4)
            for n, item in enumerate(FIRST):
                max_scores(0, n, item)
            with pe.Fori(0, NC - 1) as c:
                chunk(c, CHUNK, 0)
            chunk(NC - 1, FINAL, 3 * KT - 2)

            for k in range(EARLY, len(CLOSE)):
                close(k)
            pe.wait_ge(taken_s, len(CLOSE))
            pe.wait_ge(att_s, NC * NG + 1)
            for c in range(NC):
                pe.wait_ge(xn2_s, (c + 1) * TQ)
                for b in range(CB):
                    i = c * CB + b
                    if i >= 4:
                        pe.wait_ge(tail_a if i % 2 == 0 else tail_v, (i - 4) // 2 + 1)
                    turn_rows(i % 4, lambda t, r: xn2[:, t, b * P:(b + 1) * P], range(c * TQ, (c + 1) * TQ),
                              lambda t: P).then_inc(tail_s, 1)
                for t in range(c * TQ, (c + 1) * TQ):
                    for b in range(CB):
                        last = pe.matmul(ps[:, M_BANK + b, 0:1], xn2[:, t, b * P:(b + 1) * P], ones_sb[:, :],
                                         start=(t == 0), stop=(t == TT - 1))
            last.then_inc(sum_s, 1)
            pe.wait_ge(mean_s, 1)
            for b in range(CB):
                last = pe.matmul(ps[0:1, M_BANK + CB, 0:E], mean_sb[:, b:b + 1], wr_sb[:, b, :],
                                 start=(b == 0), stop=(b == CB - 1))
            last.then_inc(logit_s, 1)

            def ffn_up(c):
                for f in range(FT):
                    i = CB * NC + c * FT + f
                    pe.wait_ge(tail_a if i % 2 == 0 else tail_v, (i - 4) // 2 + 1)
                    for b in range(CB):
                        last = pe.matmul(ps[:, i % 4, :], w1_sb[:, b, f * P:(f + 1) * P],
                                         xn_t[:, b, c * QC:(c + 1) * QC], start=(b == 0), stop=(b == CB - 1))
                    last.then_inc(tail_s, 1)

            def ffn_down(c):
                pe.wait_ge(tail_a, (CB * NC + (c + 1) * FT) // 2)
                pe.wait_ge(tail_v, (CB * NC + (c + 1) * FT) // 2)
                for t in range(c * TQ, (c + 1) * TQ):
                    if t >= 4:
                        pe.wait_ge(out_s, t - 3)
                    for f in range(FT):
                        last = pe.matmul(ps[:, M_BANK + t % 4, 0:C], hid[:, f, t * P:(t + 1) * P],
                                         w2_sb[:, f, :], start=(f == 0), stop=(f == FT - 1))
                    last.then_inc(y_s, 1)

            pe.wait_ge(b1_s, 16)
            pe.transpose(ps[:, M_BANK + 3, 0:FT], b1_rows[:, :], ident[0:FT, 0:FT]).then_inc(b1t_s, 1)
            pe.wait_ge(w1_s, 16)
            pe.wait_ge(tail_a, CB * NC // 2)
            pe.wait_ge(tail_v, CB * NC // 2)
            for c in range(NC):
                ffn_up(c)
                if c == 1:
                    pe.wait_ge(w2_s, 16)
                    pe.wait_ge(b1c_s, 1)
                if c:
                    ffn_down(c - 1)
            ffn_down(NC - 1)


_INS = ["x", "ctx_1024", "L0_xattn_wq", "L0_xattn_bq", "L0_xattn_wk", "L0_xattn_bk", "L0_xattn_wv", "L0_xattn_bv",
        "L0_xattn_wo", "L0_xattn_bo", "L0_ffn_Wr", "L0_ffn_br", "L0_ffn_W1", "L0_ffn_b1", "L0_ffn_W2", "L0_ffn_b2"]
_OUT = ((1, 2048, 256), "float32")


def kernel(**inputs):
    import numpy as _np
    import concourse.bacc as _bacc
    from concourse import mybir as _mybir
    from concourse.bass_utils import run_bass_kernel_spmd as _run

    nc = _bacc.Bacc("TRN2", target_bir_lowering=False, num_devices=1)
    arrays, args = {}, []
    for name in _INS:
        a = _np.ascontiguousarray(inputs[name])
        arrays[f"in_{name}"] = a
        args.append(nc.dram_tensor(f"in_{name}", a.shape, _mybir.dt.from_np(a.dtype), kind="ExternalInput").ap())
    dt = _mybir.dt.from_np(_np.dtype(_OUT[1]))
    args.append(nc.dram_tensor("out_x", _OUT[0], dt, kind="ExternalOutput").ap())
    cross_attention_then_expert_ffn(nc, *args)
    r = _run(nc, [arrays], core_ids=[0])
    return r.results[0]["out_x"]
```

```python
import concourse.bass as bass
from concourse import mybir
from contextlib import ExitStack


def cross_attention_then_expert_ffn(
    nc: bass.Bass,
    x_in: bass.AP,
    ctx_in: bass.AP,
    wq_in: bass.AP,
    bq_in: bass.AP,
    wk_in: bass.AP,
    bk_in: bass.AP,
    wv_in: bass.AP,
    bv_in: bass.AP,
    wo_in: bass.AP,
    bo_in: bass.AP,
    wr_in: bass.AP,
    br_in: bass.AP,
    w1_in: bass.AP,
    b1_in: bass.AP,
    w2_in: bass.AP,
    b2_in: bass.AP,
    out: bass.AP,
):
    fp32 = mybir.dt.float32
    bf16 = mybir.dt.bfloat16
    f32r = mybir.dt.float32r
    u32 = mybir.dt.uint32
    ALU = mybir.AluOpType
    ACT = mybir.ActivationFunctionType
    AX = mybir.AxisListType

    P = 128
    TOK, C = x_in.shape[1], x_in.shape[2]
    KEYS = ctx_in.shape[1]
    H = 16
    D = C // H
    HG = 4
    NG = H // HG
    HB = P // D
    CB = C // P
    QC = 512
    NC = TOK // QC
    TT = TOK // P
    TQ = QC // P
    KT = -(-KEYS // P)
    KLAST = KEYS - (KT - 1) * P
    E, FF = w1_in.shape[0], w1_in.shape[2]
    FT = FF // P
    EPS = 1e-5
    SCALE = float(D) ** -0.5
    COL = 32

    TERMS_Q = "hmlhmh"
    TERMS_K = "hhhmml"
    NT = len(TERMS_Q)
    KR = NT * D
    ROWS = KR + 2

    KN = [401, 400, 400, 400]
    assert sum(KN) == KEYS
    KO = [sum(KN[:n]) for n in range(len(KN))]
    MW = 401
    MO = [0, 400, 800, 1200]
    assert MO[-1] + MW == KEYS and all(b - a <= MW for a, b in zip(MO, MO[1:]))

    PR = 4
    LAG = 3
    NE = 3
    SLOTS = NG * KT
    AHEAD = 8
    TURN_AFTER = 3
    ORDER = ("mvmsssms", "vmssmss")
    LATE_ORDER = "ssvss"
    HELD = 4
    TAKE_AT = -3
    BEGIN = ["ctx_t 0", "ctx_t 1", "k 0", "ctx_t 2", "x_t 0", "ctx_t 3", "k 1", "q 0", "k 2", "k 3"]
    POOL_SPLITS = [0, 2]
    STATS_AT = (13, 14, 20)
    LN_AT = 8
    INVERT_AT = (0, 4)
    KEEP = (18, 14, 12)

    ctx = ExitStack()
    with ctx:
        place = {}

        def sb(name, shape, dt=fp32):
            place[name] = -(-nc.sbuf_base // 32) * 32
            return ctx.enter_context(nc.sbuf_tensor(name, shape, dt))

        def over(region, skip, name, shape, dt):
            return nc.alloc_sbuf_tensor_at(name, shape, dt, offset=place[region] + skip)

        def sem(name):
            return ctx.enter_context(nc.semaphore(name))

        r_kq = sb("r_kq", [P, H * KEYS + NG * HG * QC], bf16)
        kpack = r_kq[:, 0:H * KEYS].rearrange("p (h k) -> p h k", h=H)
        qbuf = r_kq[:, H * KEYS:].rearrange("p (g j q) -> p g j q", g=NG, j=HG)
        hid = over("r_kq", 0, "hid", [P, 2, 2, FT, QC], f32r)
        VW = D + 1
        v_all = sb("v_all", [P, KT, H * VW + COL - VW])
        r_p = sb("r_p", [P, PR * HG * QC])
        probs = r_p[:, :].rearrange("p (s j q) -> p s j q", s=PR, j=HG)
        a = 0
        ctx_rows = r_p[:, a:a + KT * C].rearrange("p (t c) -> p t c", t=KT)
        STAGES = KT * C // QC
        stage = r_p[:, a:a + STAGES * QC].rearrange("p (s q) -> p s q", s=STAGES)
        a += KT * C
        ctx_t = r_p[:, a:a + CB * KEYS].rearrange("p (b k) -> p b k", b=CB)
        a += CB * KEYS
        w_qkv = r_p[:, a:a + 3 * CB * C].rearrange("p (w b n) -> p w b n", w=3, b=CB)
        a += 3 * CB * C
        assert a <= PR * HG * QC
        assert 2 * (CB * FF + FT * C) <= PR * HG * QC
        w1_sb = r_p[:, 0:CB * FF].rearrange("p (b f) -> p b f", b=CB)
        w2_sb = r_p[:, CB * FF:CB * FF + FT * C].rearrange("p (f c) -> p f c", f=FT)
        w1_low = over("r_p", 0, "w1_low", [P, CB, FF], f32r)
        w2_low = over("r_p", 4 * CB * FF, "w2_low", [P, FT, C], f32r)
        w1_high = over("r_p", 4 * (CB * FF + FT * C), "w1_high", [P, CB, FF], f32r)
        w2_high = over("r_p", 4 * (2 * CB * FF + FT * C), "w2_high", [P, FT, C], f32r)
        r_q = sb("r_q", [P, 3 * CB * TOK], bf16)
        q_part = r_q[:, :].rearrange("p (s b t) -> p s b t", s=3, b=CB)
        xn2 = r_q[:, 0:2 * TT * C].bitcast(fp32).rearrange("p (t c) -> p t c", t=TT)
        x_low = over("r_q", 0, "x_low", [P, NC, CB, QC], f32r)
        r_c = sb("r_c", [P, CB * TOK + NG * QC])
        k_part = r_c[:, :].bitcast(bf16)[:, 0:3 * CB * KEYS].rearrange("p (s b k) -> p s b k", s=3, b=CB)
        att = r_c[:, 0:CB * TOK].rearrange("p (b t) -> p b t", b=CB)
        hid_raw = r_c[:, 0:4 * QC].rearrange("p (s q) -> p s q", s=4)
        att_raw = r_c[:, CB * TOK:].rearrange("p (g q) -> p g q", g=NG)
        xs = sb("xs", [P, TT, C])
        xn_t = sb("xn_t", [P, CB, TOK])
        den = xn_t[0:H, 0, :]
        x_high = over("xn_t", 0, "x_high", [P, CB, TOK], f32r)
        sel = sb("sel", [H, CB, P])
        wo_sb = sb("wo_sb", [P, CB, C])
        ident = sb("ident", [P, P])
        ident_b = sb("ident_b", [P, P], bf16)
        bq_sb = sb("bq_sb", [P, CB])
        bk_sb = sb("bk_sb", [P, CB])
        b_row = sb("b_row", [P, C])
        b1_sb = sb("b1_sb", [P, FT])
        b1_rows = sb("b1_rows", [FT, P])
        wr_sb = sb("wr_sb", [P, CB, E])
        br_sb = sb("br_sb", [1, E])
        st = sb("st", [P, TT, 6])
        mv = sb("mv", [P, TT, 2])
        sd = sb("sd", [P, TT])
        rstd = sb("rstd", [P, TT])
        eps_sb = sb("eps_sb", [P, 1])
        half_max = sb("half_max", [P, NG, HG * TQ, 2])
        neg = sb("neg", [P, NG, HG * TQ])
        neg_part = sb("neg_part", [P, NG, 2, HG * TQ], bf16)
        neg_rows = sb("neg_rows", [2 * HG * TQ, NG, P], bf16)
        tok_st = sb("tok_st", [P, CB, NC, 6])
        tok_mv = sb("tok_mv", [P, CB, 2])
        warm = sb("warm", [P, 1])
        logits = sb("logits", [1, E])
        top8 = sb("top8", [1, 8])
        top_at = sb("top_at", [1, 8], u32)

        k_dram = nc.dram_tensor("k_terms", (C, NT, KEYS), bf16, kind="Internal").ap()
        q_dram = nc.dram_tensor("q_terms", (C, NT, TOK), bf16, kind="Internal").ap()

        ps = ctx.enter_context(nc.psum_tensor("ps", [P, 8, 512], fp32))
        V_BANK = NE
        M_BANK = 4

        ctx_in_s = [sem(f"ctx_loaded{n}") for n in range(-(-KT // 4))]
        wk_s = sem("wk_loaded")
        wv_s = sem("wv_loaded")
        wq_s = sem("wq_loaded")
        x_s = [sem(f"x_loaded{n}") for n in range(NC)]
        small_s = sem("small_loaded")
        wo_s = sem("wo_loaded")
        xr_s = sem("x_reloaded")
        ident_s = sem("ident_ready")
        sel_s = sem("selection_half_ready")
        fills_s = sem("fills_ready")
        v_s = sem("v_biased")
        krows_s = sem("rows_of_ones_ready")
        dve_s = sem("dve_steps")
        pre_s = sem("pre_products")
        pre_a = sem("pre_taken_act")
        pre_v = sem("pre_taken_dve")
        stats_s = sem("stats_ready")
        sqrt_s = sem("sqrt_ready")
        xn_v = sem("xn_ready_dve")
        rstd_s = sem("rstd_ready")
        high_s = sem("high_part_ready")
        parts_v = sem("parts_ready_dve")
        parts_p = sem("parts_ready_pool")
        mid_s = sem("pool_split_steps")
        middle_s = sem("middle_part_ready")
        kstored_s = [sem(f"k_stored{g}") for g in range(NG)]
        qout_s = [sem(f"q_parts_stored{n}") for n in range(NC)]
        q_s = [sem(f"q_loaded{g}") for g in range(NG)]
        rows_s = [sem(f"max_rows_loaded{g}") for g in range(NG)]
        left_s = [sem(f"region_left{g}") for g in range(NG)]
        den_s = [sem(f"last_denominators_moved{g}") for g in range(NG)]
        score_s = sem("scores_ready")
        prob_s = sem("probs_ready")
        pv_s = sem("pv_done")
        att_s = sem("att_taken")
        mrow_s = sem("max_scores_ready")
        max_s = sem("max_scores_taken")
        neg_s = sem("neg_max_steps")
        split_s = sem("neg_max_split")
        rec_s = sem("rden_ready")
        xb_s = sem("residual_biased")
        close_s = sem("close_products")
        taken_s = sem("close_taken")
        xn2_s = sem("xn2_ready")
        turned_s = sem("xn2_turned")
        warm_s = sem("root_table_loaded")
        share_s = sem("shares_of_mean_ready")
        last_turn_s = sem("last_chunk_turns")
        low_s = sem("low_parts_of_xn2_ready")
        up_s = sem("hidden_products")
        hidden_s = sem("hidden_ready")
        hid_high_s = sem("hidden_high_ready")
        hid_low_s = sem("hidden_low_ready")
        w1h_s = sem("w1_high_ready")
        w1l_s = sem("w1_low_ready")
        w2h_s = sem("w2_high_ready")
        w2l_s = sem("w2_low_ready")
        mean_s = sem("mean_ready")
        logit_s = sem("logits_ready")
        top_s = sem("top_ready")
        w1_s = [sem(f"w1_loaded{k}") for k in range(3)]
        b1_s = sem("b1_loaded")
        b1t_s = sem("b1_turned")
        b1c_s = sem("b1_column_ready")
        w2_s = sem("w2_loaded")
        b2_s = sem("b2_loaded")
        xb2_s = sem("residual2_biased")
        y_s = sem("y_products")
        out_s = sem("out_ready")
        stored_s = sem("stored")

        block = ctx.enter_context(nc.Block())

        ctx_groups = [range(4 * n, min(4 * n + 4, KT)) for n in range(-(-KT // 4))]

        PRE = []
        for item in BEGIN:
            kind, n = item.split()
            PRE += [(kind, int(n), b) for b in range(CB) if b == 0 or kind in ("ctx_t", "x_t")]
        NEED = len(PRE)
        PRE += [("k", n, 1) for n in range(len(KN))] + [("v", n, 0) for n in range(KT)]
        PRE += [("x_t", 1, b) for b in range(CB)]
        GAP = len(PRE)
        PRE += [("q", 0, 1)]
        for n in range(1, NC):
            PRE += [("q", n, 0)] + [("x_t", n + 1, b) for b in range(CB) if n + 1 < NC] + [("q", n, 1)]

        def pre_bank(i):
            return i % 8 if i < GAP else (i - GAP) % 4

        def bank_before(i):
            return max((j for j in range(i) if pre_bank(j) == pre_bank(i)), default=None)

        def by_act(item):
            kind, n, b = item
            return not (b == 1 and (kind == "ctx_t" and n or kind == "x_t" and n == 0))

        def taken_before(i, act):
            return sum(by_act(x) == act for x in PRE[:i + 1])

        def pre_at(kind, n, b):
            return PRE.index((kind, n, b))

        def wait_taken(eng, i):
            act = by_act(PRE[i])
            eng.wait_ge(pre_a if act else pre_v, taken_before(i, act))

        STAGED = [x for x in PRE if x[0] in ("k", "q")]
        SHARED = STAGED.index(("q", 0, 1))
        BY_POOL = POOL_SPLITS + list(range(SHARED, len(STAGED)))

        def wait_split(eng, i):
            pool = i in BY_POOL
            eng.wait_ge(parts_p if pool else parts_v, sum((x in BY_POOL) == pool for x in range(i + 1)))

        def plan(first, last):
            items, turn, wait = [], None, 0
            for i in range(first, last):
                n, t, half = i // (2 * TQ), i // 2 % TQ, i % 2
                items.append((n // HG, n % HG, t, half))
                if turn is not None:
                    wait -= 1
                    if wait == 0:
                        items.append((turn, "turn"))
                        turn = None
                if i % (2 * TQ * HG) == 2 * TQ * HG - 1:
                    turn, wait = n // HG, TURN_AFTER
            if turn is not None:
                items.append((turn, "turn"))
            return items

        UNIT = HG * TQ * 2
        assert AHEAD >= TURN_AFTER
        FIRST = plan(0, UNIT + AHEAD)
        CHUNK = plan(UNIT + AHEAD, UNIT + AHEAD + NG * UNIT)
        FINAL = plan(UNIT + AHEAD, NG * UNIT)
        NFIRST, NCHUNK = len(FIRST), len(CHUNK)
        assert NCHUNK % 2 == 0

        def m_bank(n):
            return M_BANK + 2 * (n % 2)

        FIRST_ROOT, TAIL0 = (NC - 2) * TQ, (NC - 1) * TQ
        CLOSE = [("spread", 0, 0), ("spread", 0, 1)]
        for n in range(NC - 1):
            if n + 1 < NC - 1:
                CLOSE += [("spread", n + 1, b) for b in range(CB)]
            CLOSE += [("project", t, 0) for t in range(n * TQ, (n + 1) * TQ)]
        CLOSE += [("turn", n, b) for n in range(NC - 2) for b in range(CB)]
        EARLY = len(CLOSE)
        for t in range(TAIL0, TT + 1):
            CLOSE += [("spread_tile", t, 0)] if t < TT else []
            CLOSE += [("turn", NC - 2, b) for b in range(CB) if t == TT]
            CLOSE += [("project", t - 1, 0)] if t > TAIL0 else []
        MAXED, CLOSE_AT, ROOT_AT = 3 * KT - 2, 3 * KT - 1, 4 * KT - 5

        def taken_before_close(k):
            return sum(x[0] != "turn" for x in CLOSE[:k])

        W1_PIECES = [(0, P), (P, FF // 2), (FF // 2, FF)]
        W2_PIECES = [(0, FT // 2), (FT // 2, FT)]

        def turn_at(items, unit):
            return items.index((unit, "turn"))

        def turned_keys(n):
            return sum(min(P, KEYS - t * P) for t in ctx_groups[n])

        def span(kind, n):
            return (KO[n], KN[n]) if kind == "k" else (n * QC, QC)

        @block.sync
        def _(sp):
            xr = x_in[0].rearrange("(t p) c -> p t c", p=P)

            def load_x(n):
                sp.dma_start(xs[:, n * TQ:(n + 1) * TQ, :], xr[:, n * TQ:(n + 1) * TQ, :]).then_inc(x_s[n], 16)

            def load_ctx(n):
                tiles = ctx_groups[n]
                whole = [t for t in tiles if (t + 1) * P <= KEYS]
                if whole:
                    sp.dma_start(ctx_rows[:, whole[0]:whole[-1] + 1, :],
                                 ctx_in[0, whole[0] * P:(whole[-1] + 1) * P, :].rearrange("(t p) c -> p t c", p=P)
                                 ).then_inc(ctx_in_s[n], 16)
                if len(whole) < len(tiles):
                    sp.dma_start(ctx_rows[0:KLAST, KT - 1, :],
                                 ctx_in[0, (KT - 1) * P:KEYS, :]).then_inc(ctx_in_s[n], 16)

            load_ctx(0)
            load_x(0)
            load_ctx(1)
            sp.dma_start(w_qkv[:, 1, :, :], wk_in.rearrange("(b p) n -> p b n", p=P)).then_inc(wk_s, 16)
            load_ctx(2)
            load_ctx(3)
            sp.dma_start(w_qkv[:, 0, :, :], wq_in.rearrange("(b p) n -> p b n", p=P)).then_inc(wq_s, 16)
            sp.dma_start(w_qkv[:, 2, :, :], wv_in.rearrange("(b p) n -> p b n", p=P)).then_inc(wv_s, 16)
            for n in range(1, NC):
                load_x(n)
            sp.dma_start(wo_sb[:, :, :], wo_in.rearrange("(b p) n -> p b n", p=P)).then_inc(wo_s, 16)

            def runs(terms):
                return [("hml".index(p), terms.index(p), terms.count(p)) for p in "hml"]

            def store_k(b, part, rows, stored):
                _, t, count = runs(TERMS_K)[part]
                sp.dma_start(k_dram[b * P + rows.start:b * P + rows.stop, t:t + count, :],
                             k_part[rows, part:part + 1, b, :].broadcast_to([rows.stop - rows.start, count, KEYS])
                             ).then_inc(stored, 16)

            def load_k(g):
                sp.dma_start(kpack[0:KR, g * HG:(g + 1) * HG, :],
                             k_dram[g * HG * D:(g + 1) * HG * D, :, :].rearrange("(j d) t k -> (d t) j k", j=HG)
                             ).then_inc(left_s[g], 16)

            def store_q(n, b):
                wait_split(sp, STAGED.index(("q", n, b)))
                cols, rows = slice(n * QC, (n + 1) * QC), slice(b * P, (b + 1) * P)
                for t, parts in ((0, 3), (3, 2), (5, 1)):
                    sp.dma_start(q_dram[rows, t:t + parts, cols], q_part[:, 0:parts, b, cols]).then_inc(qout_s[n], 16)

            def load_q(g, col):
                src = q_dram[g * HG * D:(g + 1) * HG * D, :, bass.ds(col, QC)]
                sp.dma_start(qbuf[0:KR, g, :, :], src.rearrange("(j d) t q -> (d t) j q", j=HG)).then_inc(q_s[g], 16)

            def load_rows(g):
                for s in range(2):
                    sp.dma_start(qbuf[KR + s:KR + s + 1, g, :, :].rearrange("a j (t q) -> a (j t) q", t=TQ),
                                 neg_rows[s * HG * TQ:(s + 1) * HG * TQ, g, :]).then_inc(rows_s[g], 16)

            def move_att(g, col, last):
                b, r = divmod(g * HG, HB)
                sp.dma_start(den[g * HG:(g + 1) * HG, bass.ds(col, QC)],
                             att_raw[D::COL, g, :]).then_inc(den_s[g] if last else left_s[g], 16)
                for j in range(HG):
                    sp.dma_start(att[(r + j) * D:(r + j + 1) * D, b, bass.ds(col, QC)],
                                 att_raw[j * COL:j * COL + D, g, :]).then_inc(left_s[g], 16)

            for b in range(CB):
                groups = range(b * HB // HG, (b + 1) * HB // HG)
                if b == 0:
                    store_q(0, b)
                sp.wait_ge(high_s, STAGED.index(("k", len(KN) - 1, b)) + 1)
                half = [slice(k * HG * D, (k + 1) * HG * D) for k in range(len(groups))]
                store_k(b, 0, half[0], kstored_s[groups[0]])
                for n in range(len(KN)):
                    wait_split(sp, STAGED.index(("k", n, b)))
                for part in (1, 2):
                    store_k(b, part, half[0], kstored_s[groups[0]])
                store_k(b, 0, half[1], kstored_s[groups[1]])
                sp.wait_ge(kstored_s[groups[0]], 48)
                load_k(groups[0])
                if b == 0:
                    sp.wait_ge(qout_s[0], 48)
                    load_q(groups[0], 0)
                for part in (1, 2):
                    store_k(b, part, half[1], kstored_s[groups[1]])
                sp.wait_ge(kstored_s[groups[1]], 48)
                load_k(groups[1])
                if b == 0:
                    load_q(groups[1], 0)
            store_q(0, 1)
            sp.wait_ge(qout_s[0], 96)
            for g in range(HB // HG, NG):
                load_q(g, 0)
            sp.wait_ge(max_s, turn_at(FIRST, 0) + 1)
            load_rows(0)
            for n in range(1, NC):
                for b in range(CB):
                    store_q(n, b)
            for n in range(1, NC):
                sp.wait_ge(qout_s[n], CB * 48)
            for g in range(NG):
                sp.wait_ge(left_s[g], 16)

            def chunk(c, last):
                for g in range(NG):
                    if g:
                        if not last:
                            sp.wait_ge(score_s, c * (SLOTS * HG) + g * KT * HG)
                            load_q(g - 1, c * QC + QC)
                        sp.wait_ge(att_s, c * NG + g + 1)
                        move_att(g - 1, c * QC, last)
                    if not (last and g == NG - 1):
                        sp.wait_ge(max_s, c * NCHUNK + NFIRST + turn_at(FINAL if last else CHUNK, g + 1) + 1)
                        load_rows((g + 1) % NG)
                if not last:
                    sp.wait_ge(score_s, c * (SLOTS * HG) + SLOTS * HG)
                    load_q(NG - 1, c * QC + QC)
                sp.wait_ge(att_s, c * NG + NG + 1)
                move_att(NG - 1, c * QC, last)

            with sp.Fori(0, NC - 1) as c:
                chunk(c, False)
            chunk(NC - 1, True)

            sp.wait_ge(pv_s, NC * SLOTS + 1)
            sp.wait_ge(top_s, 1)
            e = sp.value_load(top_at[0:1, 0:1], min_val=0, max_val=E - 1)
            w1_dyn = w1_in[bass.ds(e, 1), :, :].rearrange("a (b p) f -> p (a b) f", p=P)
            for k, (f0, f1) in enumerate(W1_PIECES):
                sp.dma_start(w1_sb[:, :, f0:f1], w1_dyn[:, :, f0:f1]).then_inc(w1_s[k], 16)
                if k == 0:
                    sp.dma_start(b1_rows[:, :],
                                 b1_in[bass.ds(e, 1), :].rearrange("a (f p) -> (a f) p", p=P)).then_inc(b1_s, 16)
            sp.dma_start(w2_sb, w2_in[bass.ds(e, 1), :, :].rearrange("a (f p) n -> p (a f) n", p=P)).then_inc(w2_s, 16)
            sp.wait_ge(xb_s, TT)
            sp.dma_start(b_row[:, :], b2_in[bass.ds(e, 1), :].broadcast_to([P, C])).then_inc(b2_s, 16)
            outr = out[0].rearrange("(t p) c -> p t c", p=P)
            for t in range(TT):
                sp.wait_ge(out_s, t + 1)
                sp.dma_start(outr[:, t, :], xs[:, t, :]).then_inc(stored_s, 16)
            sp.wait_ge(stored_s, TT * 16)

        @block.gpsimd
        def _(pool):
            pool.memset(ident[:, :], 0.0).then_inc(ident_s, 1)
            pool.memset(ident_b[:, :], 0.0).then_inc(ident_s, 1)
            pool.wait_ge(ident_s, 2)
            for m in (ident, ident_b):
                pool.affine_select(out=m[:, :], in_=m[:, :], compare_op=ALU.not_equal, fill=1.0, base=0,
                                   pattern=[[-1, P]], channel_multiplier=1).then_inc(ident_s, 1)
            pool.memset(sel[:, :, :], 1.0).then_inc(ident_s, 1)
            for b in range(CB):
                s_b = sel[:, b, :]
                pool.wait_ge(ident_s, 5 + b)
                pool.affine_select(out=s_b, in_=s_b, compare_op=ALU.is_ge, fill=0.0, base=D * b * HB,
                                   pattern=[[1, P]], channel_multiplier=-D).then_inc(sel_s, 1)
                pool.wait_ge(sel_s, b + 1)
                pool.affine_select(out=s_b, in_=s_b, compare_op=ALU.is_ge, fill=0.0, base=D - 1 - D * b * HB,
                                   pattern=[[-1, P]], channel_multiplier=D).then_inc(ident_s, 1)
            pool.memset(eps_sb[:, :], EPS).then_inc(fills_s, 1)
            pool.wait_ge(fills_s, 1)
            pool.memset(kpack[KR:ROWS, 0, :], 1.0).then_inc(fills_s, 1)
            pool.wait_ge(fills_s, 2)
            pool.dma_start(kpack[KR:ROWS, 1:H, :],
                           kpack[KR:ROWS, 0:1, :].broadcast_to([ROWS - KR, H - 1, KEYS])).then_inc(krows_s, 16)
            pool.memset(v_all[:, :, :], 1.0).then_inc(fills_s, 1)
            pool.wait_ge(fills_s, 3)
            for k, i in enumerate(BY_POOL[:BY_POOL.index(SHARED)]):
                kind, n, b = STAGED[i]
                o, w = span(kind, n)
                part = k_part if kind == "k" else q_part
                piece = stage[:, i % STAGES, 0:w]
                pool.wait_ge(high_s, i + 1)
                pool.tensor_tensor(piece, piece, part[:, 0, b, o:o + w], ALU.subtract).then_inc(mid_s, 1)
                pool.wait_ge(mid_s, 2 * k + 1)
                pool.tensor_copy(part[:, 1, b, o:o + w], piece).then_inc(mid_s, 1)
                pool.wait_ge(mid_s, 2 * k + 2)
                pool.tensor_tensor(part[:, 2, b, o:o + w], piece, part[:, 1, b, o:o + w],
                                   ALU.subtract).then_inc(parts_p, 1)
            pool.wait_ge(small_s, 80)
            for n in range(KT):
                rows = P if n < KT - 1 else KLAST
                v = v_all[0:rows, n, 0:H * VW].rearrange("p (h w) -> p h w", w=VW)[:, :, 0:D]
                wait_taken(pool, pre_at("v", n, 0))
                pool.tensor_tensor(v, v, b_row[0:rows, :].rearrange("p (h d) -> p h d", h=H), ALU.add).then_inc(v_s, 1)
            for i in range(SHARED, len(STAGED) + 1):
                if i < len(STAGED):
                    kind, n, b = STAGED[i]
                    o, w = span(kind, n)
                    piece = stage[:, i % STAGES, 0:w]
                    pool.wait_ge(high_s, i + 1)
                    pool.tensor_tensor(piece, piece, q_part[:, 0, b, o:o + w], ALU.subtract).then_inc(mid_s, 1)
                if i > SHARED:
                    kind, n, b = STAGED[i - 1]
                    o, w = span(kind, n)
                    pool.wait_ge(middle_s, i - SHARED)
                    pool.tensor_tensor(q_part[:, 2, b, o:o + w], stage[:, (i - 1) % STAGES, 0:w],
                                       q_part[:, 1, b, o:o + w], ALU.subtract).then_inc(parts_p, 1)
            pool.wait_ge(pre_s, len(PRE))
            pool.dma_start(xs[:, :, :], x_in[0].rearrange("(t p) c -> p t c", p=P)).then_inc(xr_s, 16)
            pool.wait_ge(v_s, KT)
            pool.dma_start(b_row[:, :], bo_in.partition_broadcast(P)).then_inc(xr_s, 16)
            pool.wait_ge(xr_s, 32)
            for t in range(TT):
                pool.tensor_tensor(xs[:, t, :], xs[:, t, :], b_row[:, :], ALU.add).then_inc(xb_s, 1)

            pool.wait_ge(b2_s, 16)
            pool.wait_ge(xn2_s, TT)
            for t in range(TT):
                pool.tensor_tensor(xs[:, t, :], xs[:, t, :], b_row[:, :], ALU.add).then_inc(xb2_s, 1)

        @block.scalar
        def _(act):
            act.dma_start(bk_sb[:, :], bk_in.rearrange("(b p) -> p b", p=P),
                          allow_slow_non_contiguous=True).then_inc(small_s, 16)
            act.dma_start(bq_sb[:, :], bq_in.rearrange("(b p) -> p b", p=P),
                          allow_slow_non_contiguous=True).then_inc(small_s, 16)
            act.dma_start(b_row[:, :], bv_in.partition_broadcast(P)).then_inc(small_s, 16)
            act.dma_start(wr_sb[:, :, :], wr_in.rearrange("(b p) e -> p b e", p=P)).then_inc(small_s, 16)
            act.dma_start(br_sb[:, :], br_in.rearrange("(a e) -> a e", a=1)).then_inc(small_s, 16)
            act.wait_ge(fills_s, 1)
            act.activation(warm[:, :], eps_sb[:, :], ACT.Sqrt).then_inc(warm_s, 1)

            def middle(i):
                kind, n, b = STAGED[i]
                o, w = span(kind, n)
                act.wait_ge(mid_s, 2 * BY_POOL.index(SHARED) + i - SHARED + 1)
                act.activation(q_part[:, 1, b, o:o + w], stage[:, i % STAGES, 0:w], ACT.Copy).then_inc(middle_s, 1)

            staged = 0
            for i, (kind, n, b) in enumerate(PRE):
                if i == pre_at("k", 0, 0):
                    act.wait_ge(stats_s, TQ)
                    act.activation(sd[:, 0:TQ], mv[:, 0:TQ, 1], ACT.Sqrt, bias=eps_sb[:, 0:1]).then_inc(sqrt_s, 1)
                    act.wait_ge(small_s, 80)
                if i == NEED + LN_AT - 1:
                    act.wait_ge(stats_s, TT)
                    act.activation(sd[:, TQ:TT], mv[:, TQ:TT, 1], ACT.Sqrt, bias=eps_sb[:, 0:1]).then_inc(sqrt_s, 1)
                if not by_act(PRE[i]):
                    continue
                act.wait_ge(pre_s, i + 1)
                bank = pre_bank(i)
                if kind == "ctx_t":
                    act.activation(ctx_t[:, b, n * 512:n * 512 + turned_keys(n)], ps[:, bank, 0:turned_keys(n)],
                                   ACT.Copy).then_inc(pre_a, 1)
                elif kind == "x_t":
                    act.activation(xn_t[:, b, n * QC:(n + 1) * QC], ps[:, bank, :], ACT.Copy).then_inc(pre_a, 1)
                elif kind == "v":
                    rows = P if n < KT - 1 else KLAST
                    if n == 0:
                        act.wait_ge(fills_s, 3)
                    act.activation(v_all[0:rows, n, 0:H * VW].rearrange("p (h w) -> p h w", w=VW)[:, :, 0:D],
                                   ps[0:rows, bank, 0:C].rearrange("p (h d) -> p h d", h=H),
                                   ACT.Copy).then_inc(pre_a, 1)
                else:
                    part, bias = (k_part, bk_sb) if kind == "k" else (q_part, bq_sb)
                    o, w = span(kind, n)
                    if staged >= STAGES:
                        wait_split(act, staged - STAGES)
                    act.activation(stage[:, staged % STAGES, 0:w], ps[:, bank, 0:w], ACT.Identity,
                                   bias=bias[:, b:b + 1]).then_inc(pre_a, 1)
                    act.wait_ge(pre_a, taken_before(i, True))
                    act.activation(part[:, 0, b, o:o + w], stage[:, staged % STAGES, 0:w], ACT.Copy).then_inc(high_s, 1)
                    if staged > SHARED:
                        middle(staged - 1)
                    staged += 1
            middle(staged - 1)
            act.wait_ge(parts_p, len(BY_POOL))
            act.wait_ge(parts_v, len(STAGED) - len(BY_POOL))
            act.sem_inc(att_s, 1)

            def take_att(c, g):
                act.wait_ge(pv_s, c * SLOTS + (g + 1) * KT + 1)
                act.wait_ge(left_s[g], c * (HG + 1) * 16 + 16)
                act.activation(att_raw[:, g, :], ps[:, V_BANK, :], ACT.Copy).then_inc(att_s, 1)

            def root(t0, t1):
                act.wait_ge(stats_s, TT + t1)
                act.activation(sd[:, t0:t1], mv[:, t0:t1, 1], ACT.Sqrt, bias=eps_sb[:, 0:1]).then_inc(sqrt_s, 1)

            def chunk(c, last):
                for s in range(SLOTS):
                    g, kt = divmod(s, KT)
                    rows = P if kt < KT - 1 else KLAST
                    if last and s == ROOT_AT:
                        root(0, FIRST_ROOT)
                    act.wait_ge(pv_s, c * SLOTS + max(0, s - PR + 1) + 1)
                    for j in range(HG):
                        e = s * HG + j
                        if g and (kt, j) == (LAG + TAKE_AT // HG, TAKE_AT % HG):
                            take_att(c, g - 1)
                        act.wait_ge(score_s, c * (SLOTS * HG) + e + 1)
                        act.activation(probs[0:rows, s % PR, j, :], ps[0:rows, e % NE, :], ACT.Exp,
                                       scale=SCALE).then_inc(prob_s, 1)
                take_att(c, NG - 1)

            with act.Fori(0, NC - 1) as c:
                chunk(c, False)
            chunk(NC - 1, True)

            act.wait_ge(warm_s, 1)
            act.activation(warm[:, :], eps_sb[:, :], ACT.Sqrt).then_inc(warm_s, 1)
            root(FIRST_ROOT, TAIL0)
            for b in range(CB):
                k = CLOSE.index(("turn", NC - 2, b))
                act.wait_ge(close_s, k + 1)
                act.activation(x_high[:, b, (NC - 2) * QC:(NC - 1) * QC], ps[:, M_BANK + k % 4, :],
                               ACT.Copy).then_inc(turned_s, 1)
            root(TAIL0, TT)
            for b in range(CB):
                act.wait_ge(last_turn_s, b + 1)
                act.activation(x_high[:, b, (NC - 1) * QC:TOK], ps[:, b, :], ACT.Copy).then_inc(turned_s, 1)
            for k, (f0, f1) in enumerate(W1_PIECES):
                act.wait_ge(w1_s[k], 16)
                act.activation(w1_high[:, :, f0:f1], w1_sb[:, :, f0:f1], ACT.Copy).then_inc(w1h_s, 1)

            def high(i):
                c, f = divmod(i, FT)
                act.wait_ge(hidden_s, i + 1)
                if c >= 2:
                    act.wait_ge(y_s, (c - 1) * TQ)
                act.activation(hid[:, 0, c % 2, f, :], hid_raw[:, i % 4, :], ACT.Copy).then_inc(hid_high_s, 1)

            act.wait_ge(b1c_s, 1)
            for i in range(NC * FT):
                c, f = divmod(i, FT)
                if i == FT:
                    for f0, f1 in W2_PIECES:
                        act.wait_ge(w2_s, 16)
                        act.activation(w2_high[:, f0:f1, :], w2_sb[:, f0:f1, :], ACT.Copy).then_inc(w2h_s, 1)
                act.wait_ge(up_s, i + 1)
                if i >= 4:
                    act.wait_ge(hid_low_s, i - 3)
                act.activation(hid_raw[:, i % 4, :], ps[:, i % 4, :], ACT.Relu,
                               bias=b1_sb[:, f:f + 1]).then_inc(hidden_s, 1)
                if i:
                    high(i - 1)
            high(NC * FT - 1)

        @block.vector
        def _(dve):
            steps = [0]

            def link(ins):
                steps[0] += 1
                ins.then_inc(dve_s, 1)
                dve.wait_ge(dve_s, steps[0])

            def take_pre(i):
                kind, n, b = PRE[i]
                dve.wait_ge(pre_s, i + 1)
                bank = pre_bank(i)
                if kind == "ctx_t":
                    dve.tensor_copy(ctx_t[:, b, n * 512:n * 512 + turned_keys(n)],
                                    ps[:, bank, 0:turned_keys(n)]).then_inc(pre_v, 1)
                else:
                    dve.tensor_copy(xn_t[:, b, n * QC:(n + 1) * QC], ps[:, bank, :]).then_inc(pre_v, 1)

            def split_parts(i):
                kind, n, b = STAGED[i]
                o, w = span(kind, n)
                part = k_part if kind == "k" else q_part
                s = stage[:, i % STAGES, 0:w]
                dve.wait_ge(high_s, i + 1)
                link(dve.tensor_tensor(s, s, part[:, 0, b, o:o + w], ALU.subtract))
                link(dve.tensor_copy(part[:, 1, b, o:o + w], s))
                dve.tensor_tensor(part[:, 2, b, o:o + w], s, part[:, 1, b, o:o + w],
                                  ALU.subtract).then_inc(parts_v, 1)

            def layer_stats(tiles):
                for t in tiles:
                    last = dve.bn_stats(st[:, t, :], xs[:, t, :])
                link(last)
                for t in tiles:
                    dve.bn_aggr(mv[:, t, :], st[:, t, :]).then_inc(stats_s, 1)

            dve.wait_ge(x_s[0], 16)
            layer_stats(range(TQ))
            staged = 0
            for i, item in enumerate(PRE):
                if item == ("k", 0, 0):
                    dve.wait_ge(sqrt_s, 1)
                    dve.reciprocal(rstd[:, 0:TQ], sd[:, 0:TQ]).then_inc(rstd_s, 1)
                    dve.wait_ge(rstd_s, 1)
                    for t in range(TQ):
                        dve.tensor_scalar(xs[:, t, :], xs[:, t, :], mv[:, t, 0:1], rstd[:, t:t + 1],
                                          ALU.subtract, ALU.mult).then_inc(xn_v, 1)
                if i == NEED + LN_AT:
                    dve.wait_ge(sqrt_s, 2)
                    dve.reciprocal(rstd[:, TQ:TT], sd[:, TQ:TT]).then_inc(rstd_s, 1)
                    dve.wait_ge(rstd_s, 2)
                    for t in range(TQ, TT):
                        dve.tensor_scalar(xs[:, t, :], xs[:, t, :], mv[:, t, 0:1], rstd[:, t:t + 1],
                                          ALU.subtract, ALU.mult).then_inc(xn_v, 1)
                for n in range(1, NC):
                    if i == STATS_AT[n - 1]:
                        dve.wait_ge(x_s[n], 16)
                        layer_stats(range(n * TQ, (n + 1) * TQ))
                if item[0] in ("k", "q"):
                    if staged not in BY_POOL:
                        split_parts(staged)
                    staged += 1
                elif not by_act(item):
                    take_pre(i)

            def take_max(c, n, item):
                unit, g = item[0], item[0] % NG
                dve.wait_ge(mrow_s, c * NCHUNK + n + 1)
                bank = m_bank(n)
                if item[1] == "turn":
                    dve.tensor_copy(neg_rows[:, g, :],
                                    ps[0:2 * HG * TQ, bank, 0:P // 2].bitcast(bf16)).then_inc(max_s, 1)
                    return
                _, j, t, half = item
                dve.reduce_max(half_max[:, g, j * TQ + t, half:half + 1], ps[:, bank:bank + 2, 0:MW],
                               AX.XY).then_inc(max_s, 1)
                if (j, t, half) == (HG - 1, TQ - 1, 1):
                    dve.wait_ge(max_s, c * NCHUNK + n + 1)
                    dve.tensor_reduce(neg[:, g, :], half_max[:, g, :, :], AX.X, ALU.max,
                                      negate=True).then_inc(neg_s, 1)
                    dve.wait_ge(neg_s, c * (2 * NG) + 2 * unit + 1)
                    dve.tensor_copy(neg_part[:, g, 0, :], neg[:, g, :]).then_inc(neg_s, 1)
                    dve.wait_ge(neg_s, c * (2 * NG) + 2 * unit + 2)
                    dve.tensor_tensor(neg_part[:, g, 1, :], neg[:, g, :], neg_part[:, g, 0, :],
                                      ALU.subtract).then_inc(split_s, 1)

            def invert(n, i, pieces):
                o, w = n * QC + i * (QC // pieces), QC // pieces
                dve.reciprocal(den[:, o:o + w], den[:, o:o + w]).then_inc(rec_s, 1)

            def moved(n):
                for g in range(NG):
                    dve.wait_ge(left_s[g], 16 + (n + 1) * (HG + 1) * 16 - (16 if n == NC - 1 else 0))

            for n, item in enumerate(FIRST):
                take_max(0, n, item)
            with dve.Fori(0, NC - 1) as c:
                for n, item in enumerate(CHUNK):
                    take_max(c, NFIRST + n, item)
            for n, item in enumerate(FINAL):
                take_max(NC - 1, NFIRST + n, item)
                if n % 20 == 19:
                    moved(0)
                    invert(0, n // 20, TQ)

            def normalise(t0, t1):
                link(dve.reciprocal(rstd[:, t0:t1], sd[:, t0:t1]))
                for t in range(t0, t1):
                    dve.tensor_scalar(xn2[:, t, :], xs[:, t, :], mv[:, t, 0:1], rstd[:, t:t + 1],
                                      ALU.subtract, ALU.mult).then_inc(xn2_s, 1)

            def turned_bank(n, b):
                return b if n == NC - 1 else M_BANK + CLOSE.index(("turn", n, b)) % 4

            def share(n):
                for b in range(CB):
                    if n >= NC - 2:
                        dve.wait_ge(turned_s, (n - (NC - 2)) * CB + b + 1)
                    dve.bn_stats(tok_st[:, b, n, :], ps[:, turned_bank(n, b), :]).then_inc(share_s, 1)

            def low(n):
                if n >= NC - 2:
                    dve.wait_ge(turned_s, (n - (NC - 2) + 1) * CB)
                for b in range(CB):
                    dve.tensor_tensor(x_low[:, n, b, :], ps[:, turned_bank(n, b), :],
                                      x_high[:, b, n * QC:(n + 1) * QC].bitcast(fp32), ALU.subtract).then_inc(low_s, 1)

            def turned(n):
                for b in range(CB):
                    dve.wait_ge(close_s, CLOSE.index(("turn", n, b)) + 1)
                    last = dve.tensor_copy(x_high[:, b, n * QC:(n + 1) * QC], ps[:, turned_bank(n, b), :])
                link(last)
                share(n)
                low(n)

            for k, (kind, n, b) in enumerate(CLOSE):
                for c in range(1, NC - 1):
                    if k == INVERT_AT[c - 1]:
                        moved(c)
                        for i in range(TQ):
                            invert(c, i, TQ)
                if (kind, n, b) == ("turn", 0, 0):
                    for g in range(NG):
                        dve.wait_ge(q_s[g], NC * 16)
                    dve.wait_ge(sqrt_s, 3)
                    normalise(0, FIRST_ROOT)
                if (kind, n) == ("spread_tile", TAIL0):
                    dve.wait_ge(sqrt_s, 4)
                    normalise(FIRST_ROOT, TAIL0)
                    for g in range(NG):
                        dve.wait_ge(den_s[g], 16)
                    invert(NC - 1, 0, TQ)
                if kind == "spread_tile" and n + 1 < TT:
                    invert(NC - 1, n + 1 - TAIL0, TQ)
                if kind == "turn":
                    if b == CB - 1 and n < NC - 2:
                        turned(n)
                    continue
                dve.wait_ge(close_s, k + 1)
                bank = M_BANK + k % 4
                if kind == "spread":
                    cols = slice(n * QC, (n + 1) * QC)
                    dve.tensor_tensor(att[:, b, cols], att[:, b, cols], ps[:, bank, :], ALU.mult).then_inc(taken_s, 1)
                elif kind == "spread_tile":
                    if n == TAIL0:
                        moved(NC - 1)
                    cols = slice(n * P, (n + 1) * P)
                    dve.tensor_tensor(att[:, :, cols], att[:, :, cols],
                                      ps[:, bank, 0:CB * P].rearrange("p (b q) -> p b q", b=CB),
                                      ALU.mult).then_inc(taken_s, 1)
                elif kind == "project":
                    dve.wait_ge(xb_s, n + 1)
                    dve.tensor_tensor(xs[:, n, :], ps[:, bank, 0:C], xs[:, n, :], ALU.add).then_inc(taken_s, 1)
                    dve.wait_ge(taken_s, taken_before_close(k) + 1)
                    link(dve.bn_stats(st[:, n, :], xs[:, n, :]))
                    dve.bn_aggr(mv[:, n, :], st[:, n, :]).then_inc(stats_s, 1)
            share(NC - 2)
            dve.wait_ge(sqrt_s, 5)
            normalise(TAIL0, TT)
            low(NC - 2)
            share(NC - 1)
            dve.wait_ge(share_s, NC * CB)
            for b in range(CB):
                dve.bn_aggr(tok_mv[:, b, :], tok_st[:, b, :, :]).then_inc(mean_s, 1)
            dve.wait_ge(logit_s, 1)
            link(dve.tensor_tensor(logits[:, :], ps[0:1, V_BANK, 0:E], br_sb[:, :], ALU.add))
            link(dve.max(top8[:, :], logits[:, :]))
            dve.max_index(top_at[:, :], top8[:, :], logits[:, :]).then_inc(top_s, 1)

            def low_w1(k):
                f0, f1 = W1_PIECES[k]
                dve.wait_ge(w1h_s, k + 1)
                dve.tensor_tensor(w1_low[:, :, f0:f1], w1_sb[:, :, f0:f1], w1_high[:, :, f0:f1].bitcast(fp32),
                                  ALU.subtract).then_inc(w1l_s, 1)

            def low_w2(k):
                f0, f1 = W2_PIECES[k]
                dve.wait_ge(w2h_s, k + 1)
                dve.tensor_tensor(w2_low[:, f0:f1, :], w2_sb[:, f0:f1, :], w2_high[:, f0:f1, :].bitcast(fp32),
                                  ALU.subtract).then_inc(w2l_s, 1)

            def hidden(c):
                for f in range(FT):
                    i = c * FT + f
                    dve.wait_ge(hid_high_s, i + 1)
                    dve.tensor_tensor(hid[:, 1, c % 2, f, :], hid_raw[:, i % 4, :],
                                      hid[:, 0, c % 2, f, :].bitcast(fp32), ALU.subtract).then_inc(hid_low_s, 1)

            def result(c):
                for t in range(c * TQ, (c + 1) * TQ):
                    dve.wait_ge(y_s, t + 1)
                    dve.wait_ge(xb2_s, t + 1)
                    dve.tensor_tensor(xs[:, t, :], ps[:, M_BANK + t % 4, 0:C], xs[:, t, :],
                                      ALU.add).then_inc(out_s, 1)

            low(NC - 1)
            low_w1(0)
            dve.wait_ge(b1t_s, 1)
            dve.tensor_copy(b1_sb[:, :], ps[:, M_BANK, 0:FT]).then_inc(b1c_s, 1)
            low_w1(1)
            low_w1(2)
            for c in range(NC):
                hidden(c)
                if c == 0:
                    low_w2(0)
                    low_w2(1)
                if c:
                    result(c - 1)
            result(NC - 1)

        @block.tensor
        def _(pe):
            def turn_rows(bank, src, tiles, rows_of):
                for k, t in enumerate(tiles):
                    r = rows_of(t)
                    last = pe.transpose(ps[:, bank, k * P:k * P + r], src(t, r), ident[0:r, 0:r])
                return last

            pe.wait_ge(ident_s, 4)
            def before(i, part=None):
                kind, n, b = PRE[i]
                if not part and bank_before(i) is not None:
                    wait_taken(pe, bank_before(i))
                bank = pre_bank(i)
                if kind == "ctx_t":
                    whole = sum((t + 1) * P <= KEYS for t in ctx_groups[n])
                    pe.wait_ge(ctx_in_s[n], 16 * ((whole > 0) + (whole < len(ctx_groups[n]))))
                    last = turn_rows(bank, lambda t, r: ctx_rows[0:r, t, b * P:(b + 1) * P], ctx_groups[n],
                                     lambda t: min(P, KEYS - t * P))
                elif kind == "k":
                    pe.wait_ge(wk_s, 16)
                    o, w = span(kind, n)
                    for kb in range(CB):
                        wait_taken(pe, pre_at("ctx_t", (o + w - 1) // (4 * P), kb))
                        wait_taken(pe, pre_at("ctx_t", o // (4 * P), kb))
                    for kb in range(CB):
                        last = pe.matmul(ps[:, bank, 0:w], w_qkv[:, 1, kb, b * P:(b + 1) * P],
                                         ctx_t[:, kb, o:o + w], start=(kb == 0), stop=(kb == CB - 1))
                elif kind == "v":
                    pe.wait_ge(wv_s, 16)
                    rows = P if n < KT - 1 else KLAST
                    for kb in range(CB):
                        last = pe.matmul(ps[0:rows, bank, 0:C], ctx_t[:, kb, n * P:n * P + rows],
                                         w_qkv[:, 2, kb, :], start=(kb == 0), stop=(kb == CB - 1))
                elif kind == "x_t":
                    pe.wait_ge(xn_v, (n + 1) * TQ)
                    last = turn_rows(bank, lambda t, r: xs[:, t, b * P:(b + 1) * P],
                                     range(n * TQ, (n + 1) * TQ), lambda t: P)
                else:
                    pe.wait_ge(wq_s, 16)
                    wait_taken(pe, pre_at("x_t", n, 0))
                    wait_taken(pe, pre_at("x_t", n, 1))
                    for kb in range(CB) if part is None else [part]:
                        last = pe.matmul(ps[:, bank, :], w_qkv[:, 0, kb, b * P:(b + 1) * P],
                                         xn_t[:, kb, n * QC:(n + 1) * QC], start=(kb == 0), stop=(kb == CB - 1))
                if part != 0:
                    last.then_inc(pre_s, 1)

            def max_scores(c, n, item):
                unit, g = item[0], item[0] % NG
                if not (isinstance(c, int) and c * NCHUNK + n < 2):
                    pe.wait_ge(max_s, c * NCHUNK + n - 1)
                bank = m_bank(n)
                if item[1] == "turn":
                    pe.wait_ge(split_s, c * NG + unit + 1)
                    pe.transpose(ps[0:2 * HG * TQ, bank, 0:P // 2].bitcast(bf16),
                                 neg_part[:, g, :, :].rearrange("p s n -> p (s n)"), ident_b[:, :]).then_inc(mrow_s, 1)
                    return
                _, j, t, half = item
                if (j, t, half) == (0, 0, 0):
                    pe.wait_ge(q_s[g], c * 16 + (unit // NG + 1) * 16)
                for k in range(2):
                    o = MO[2 * half + k]
                    last = pe.matmul(ps[:, bank + k, 0:MW], qbuf[0:KR, g, j, t * P:(t + 1) * P],
                                     kpack[0:KR, g * HG + j, o:o + MW], start=True, stop=True)
                last.then_inc(mrow_s, 1)

            def scores(c, s, j):
                g, kt = divmod(s, KT)
                rows = P if kt < KT - 1 else KLAST
                if kt == 0 and j == 0:
                    pe.wait_ge(rows_s[g], c * 32 + 32)
                e = s * HG + j
                if e >= NE:
                    pe.wait_ge(prob_s, c * (SLOTS * HG) + e - NE + 1)
                pe.matmul(ps[0:rows, e % NE, :], kpack[0:ROWS, g * HG + j, kt * P:kt * P + rows],
                          qbuf[0:ROWS, g, j, :], start=True, stop=True).then_inc(score_s, 1)

            def times_v(c, s):
                g, kt = divmod(s, KT)
                rows = P if kt < KT - 1 else KLAST
                if kt == 0:
                    pe.wait_ge(att_s, c * NG + g + 1)
                pe.wait_ge(prob_s, c * (SLOTS * HG) + (s + 1) * HG)
                for j in range(HG):
                    v = v_all[0:rows, kt, (g * HG + j) * VW:(g * HG + j) * VW + COL]
                    last = pe.matmul(ps[j * COL:(j + 1) * COL, V_BANK, :], v, probs[0:rows, s % PR, j, :],
                                     start=(kt == 0), stop=(kt == KT - 1))
                last.then_inc(pv_s, 1)

            def close(k):
                kind, n, b = CLOSE[k]
                bank = M_BANK + k % 4
                if k < 4:
                    pe.wait_ge(max_s, (NC - 1) * NCHUNK + NFIRST + len(FINAL))
                elif CLOSE[k - 4][0] != "turn":
                    pe.wait_ge(taken_s, taken_before_close(k - 4) + 1)
                else:
                    pe.wait_ge(low_s, CLOSE[k - 4][1] * CB + CLOSE[k - 4][2] + 1)
                if kind == "spread":
                    pe.wait_ge(ident_s, 5 + CB)
                    pe.wait_ge(rec_s, (n + 1) * TQ)
                    last = pe.matmul(ps[:, bank, :], sel[:, b, :], den[:, n * QC:(n + 1) * QC], start=True, stop=True)
                elif kind == "spread_tile":
                    pe.wait_ge(rec_s, n + 1)
                    for b in range(CB):
                        last = pe.matmul(ps[:, bank, b * P:(b + 1) * P], sel[:, b, :], den[:, n * P:(n + 1) * P],
                                         start=True, stop=True)
                elif kind == "turn":
                    pe.wait_ge(xn2_s, (n + 1) * TQ)
                    last = turn_rows(bank, lambda t, r: xn2[:, t, b * P:(b + 1) * P],
                                     range(n * TQ, (n + 1) * TQ), lambda t: P)
                else:
                    pe.wait_ge(wo_s, 16)
                    spread = ("spread", n // TQ, CB - 1) if n < TAIL0 else ("spread_tile", n, 0)
                    pe.wait_ge(taken_s, taken_before_close(CLOSE.index(spread)) + 1)
                    for b in range(CB):
                        last = pe.matmul(ps[:, bank, 0:C], att[:, b, n * P:(n + 1) * P], wo_sb[:, b, :],
                                         start=(b == 0), stop=(b == CB - 1))
                last.then_inc(close_s, 1)

            def closed(s):
                return max(0, EARLY * (s - CLOSE_AT) // (SLOTS - CLOSE_AT))

            def chunk(c, items, late):
                done, over, held = 0, late or SLOTS, 0 if late else HELD
                both = (ORDER[0] + ORDER[1]).count("m")
                for s in range(SLOTS):
                    order = LATE_ORDER if late and s >= late else ORDER[s % 2]
                    for k, what in enumerate(order):
                        if what == "s":
                            scores(c, s, order[:k].count("s"))
                        elif what == "v" and s >= LAG:
                            times_v(c, s - LAG)
                        elif what == "m":
                            place = both * (s // 2) + (ORDER[0] * (s % 2) + order[:k]).count("m") + 1
                            upto = min(len(items), (len(items) - held) * place // (both * over // 2))
                            for n in range(done, upto):
                                max_scores(c, NFIRST + n, items[n])
                            done = max(done, upto)
                    if late:
                        for k in range(closed(s), closed(s + 1)):
                            close(k)
                for s in range(SLOTS - LAG, SLOTS):
                    upto = len(items) if s == SLOTS - 1 else done + (len(items) - done) // (SLOTS - s)
                    for n in range(done, upto):
                        max_scores(c, NFIRST + n, items[n])
                    done = upto
                    times_v(c, s)

            for i in range(GAP):
                before(i)
            for i in range(GAP - 8, GAP):
                if pre_bank(i) >= M_BANK:
                    wait_taken(pe, i)
            steps = [(i, part) for i in range(GAP, len(PRE)) for part in ([0, 1] if PRE[i][0] == "q" else [None])]
            made = 0
            for n, item in enumerate(FIRST):
                if len(item) == 4 and item[1:] == (0, 0, 0):
                    pe.wait_ge(left_s[item[0] % NG], 16)
                max_scores(0, n, item)
                upto = min(len(steps), len(steps) * (n + 1) // (len(FIRST) - 6))
                for i, part in steps[made:upto]:
                    before(i, part)
                made = upto
            for i in range(len(PRE) - 4, len(PRE)):
                wait_taken(pe, i)
            for g in range(NG):
                pe.wait_ge(left_s[g], 16)
            pe.wait_ge(krows_s, 16)
            pe.wait_ge(v_s, KT)
            pe.wait_ge(fills_s, 3)
            pe.sem_inc(pv_s, 1)
            with pe.Fori(0, NC - 1) as c:
                chunk(c, CHUNK, 0)
            chunk(NC - 1, FINAL, MAXED)

            def keep_clock(n):
                for _ in range(n):
                    pe.matmul(ps[:, NE - 1, :], kpack[0:KR, 0, 0:P], kpack[0:KR, 0, 0:512], start=True, stop=True)

            keep_clock(KEEP[0])
            for k in range(EARLY, len(CLOSE)):
                close(k)
            pe.wait_ge(att_s, NC * NG + 1)
            keep_clock(KEEP[1])
            pe.wait_ge(xn2_s, TT)
            for b in range(CB):
                turn_rows(b, lambda t, r: xn2[:, t, b * P:(b + 1) * P], range(TAIL0, TT),
                          lambda t: P).then_inc(last_turn_s, 1)
            pe.wait_ge(mean_s, CB)
            for b in range(CB):
                last = pe.matmul(ps[0:1, V_BANK, 0:E], tok_mv[:, b, 0:1], wr_sb[:, b, :],
                                 start=(b == 0), stop=(b == CB - 1))
            last.then_inc(logit_s, 1)
            keep_clock(KEEP[2])

            def ffn_up(c):
                cols = slice(c * QC, (c + 1) * QC)
                pe.wait_ge(low_s, (c + 1) * CB)
                for f in range(FT):
                    i = c * FT + f
                    if i >= 4:
                        pe.wait_ge(hidden_s, i - 3)
                    elif i == V_BANK:
                        pe.wait_ge(top_s, 1)
                    rows = slice(f * P, (f + 1) * P)
                    if c == 0:
                        piece = [f0 <= f * P < f1 for f0, f1 in W1_PIECES].index(True)
                        if f == 1:
                            pe.wait_ge(b1_s, 16)
                            pe.transpose(ps[:, M_BANK, 0:FT], b1_rows[:, :], ident[0:FT, 0:FT]).then_inc(b1t_s, 1)
                        pe.wait_ge(w1h_s, piece + 1)
                    for b in range(CB):
                        pe.matmul(ps[:, i % 4, :], w1_high[:, b, rows], x_high[:, b, cols], start=(b == 0), stop=False)
                        pe.matmul(ps[:, i % 4, :], w1_high[:, b, rows], x_low[:, c, b, :], start=False, stop=False)
                    if c == 0:
                        pe.wait_ge(w1l_s, piece + 1)
                    for b in range(CB):
                        last = pe.matmul(ps[:, i % 4, :], w1_low[:, b, rows], x_high[:, b, cols],
                                         start=False, stop=(b == CB - 1))
                    last.then_inc(up_s, 1)

            def ffn_down(c):
                pe.wait_ge(hid_high_s, (c + 1) * FT)
                pe.wait_ge(hid_low_s, (c + 1) * FT)
                for t in range(TQ):
                    if c:
                        pe.wait_ge(out_s, (c - 1) * TQ + t + 1)
                    for f in range(FT):
                        h, l = (hid[:, s, c % 2, f, t * P:(t + 1) * P] for s in range(2))
                        y = ps[:, M_BANK + t, 0:C]
                        pe.matmul(y, h, w2_high[:, f, :], start=(f == 0), stop=False)
                        pe.matmul(y, h, w2_low[:, f, :], start=False, stop=False)
                        last = pe.matmul(y, l, w2_high[:, f, :], start=False, stop=(f == FT - 1))
                    last.then_inc(y_s, 1)

            pe.wait_ge(taken_s, taken_before_close(len(CLOSE)))
            pe.wait_ge(low_s, NC * CB)
            for c in range(NC):
                ffn_up(c)
                if c == 1:
                    pe.wait_ge(w2l_s, len(W2_PIECES))
                    pe.wait_ge(w2h_s, len(W2_PIECES))
                    pe.wait_ge(b1c_s, 1)
                if c:
                    ffn_down(c - 1)
            ffn_down(NC - 1)


_INS = ["x", "ctx_1024", "L0_xattn_wq", "L0_xattn_bq", "L0_xattn_wk", "L0_xattn_bk", "L0_xattn_wv", "L0_xattn_bv",
        "L0_xattn_wo", "L0_xattn_bo", "L0_ffn_Wr", "L0_ffn_br", "L0_ffn_W1", "L0_ffn_b1", "L0_ffn_W2", "L0_ffn_b2"]
_OUT = ((1, 2048, 256), "float32")


def kernel(**inputs):
    import numpy as _np
    import concourse.bacc as _bacc
    from concourse import mybir as _mybir
    from concourse.bass_utils import run_bass_kernel_spmd as _run

    nc = _bacc.Bacc("TRN2", target_bir_lowering=False, num_devices=1)
    arrays, args = {}, []
    for name in _INS:
        a = _np.ascontiguousarray(inputs[name])
        arrays[f"in_{name}"] = a
        args.append(nc.dram_tensor(f"in_{name}", a.shape, _mybir.dt.from_np(a.dtype), kind="ExternalInput").ap())
    dt = _mybir.dt.from_np(_np.dtype(_OUT[1]))
    args.append(nc.dram_tensor("out_x", _OUT[0], dt, kind="ExternalOutput").ap())
    cross_attention_then_expert_ffn(nc, *args)
    r = _run(nc, [arrays], core_ids=[0])
    return r.results[0]["out_x"]
```
